# Optimizing a Trainium2 kernel written in Bass

```python
import numpy as np
import jax
import jax.numpy as jnp

def _softmax(x, axis=-1):
    return jax.nn.softmax(x, axis=axis)

def _gelu(x):
    return jax.nn.gelu(x, approximate=True)

def _silu(x):
    return jax.nn.silu(x)

def _sigmoid(x):
    return jax.nn.sigmoid(x)

def _layernorm(x, axis=-1, eps=1e-05):
    m = jnp.mean(x, axis=axis, keepdims=True)
    v = jnp.var(x, axis=axis, keepdims=True)
    return (x - m) / jnp.sqrt(v + eps)

def _scatter_add(tgt, idx, src, axis=0):
    return tgt.at[idx].add(src)

def _segment_sum(src, seg, n):
    return jax.ops.segment_sum(src, seg, n)
kernel_name = 'mk_flamingo_gated_d1_seqx_r8_e848cc'

def setup_inputs(seed: int=0):
    np.random.seed(seed)
    _w = jnp.asarray

    def _rec_inputs():
        import jax
        import jax.numpy as jnp
        _rk = jax.random.key(seed)
        x = 4.136e-05 + 0.9999 * jax.random.normal(jax.random.fold_in(_rk, 1), (32, 128, 128), jnp.float32)
        _lenS = 128 - jax.random.randint(jax.random.fold_in(_rk, 7), (32,), 0, max(1, 128 // 4) + 1, jnp.int32)
        _lenS2 = 128 - jax.random.randint(jax.random.fold_in(_rk, 8), (32,), 0, max(1, 128 // 4) + 1, jnp.int32)
        _ctx_2048P = jax.random.normal(jax.random.fold_in(_rk, 11), (32, 16, 256), jnp.float32)
        _ctx_2048c = jax.random.dirichlet(jax.random.fold_in(_rk, 511), 0.3 * jnp.ones((16,), jnp.float32), (32, 128))
        _ctx_2048t = jnp.einsum('bsk,bkd->bsd', _ctx_2048c, _ctx_2048P)
        _ctx_2048t = _ctx_2048t * jax.lax.rsqrt(jnp.mean(jnp.square(_ctx_2048t)) + 1e-12) * 0.953939
        ctx_2048 = -0.000392918 + 0.999932 * (_ctx_2048t + 0.3 * jax.random.normal(jax.random.fold_in(_rk, 611), (32, 128, 256), jnp.float32))
        itok_Bx1_68_817 = jax.random.randint(jax.random.fold_in(_rk, 12), (32, 1), 68, 818, jnp.int32)
        _g = jax.random.normal(jax.random.fold_in(_rk, 9001), (2, 1), jnp.float32)
        _g = jnp.sign(_g) * jnp.maximum(jnp.abs(_g), 1.0) + (_g == 0) * 1.0
        g_xattn = _g[0]
        g_ffn = _g[1]
        return (x, ctx_2048, itok_Bx1_68_817, g_xattn, g_ffn)
    x, ctx_2048, itok_Bx1_68_817, g_xattn, g_ffn = _rec_inputs()

    def _L0_xattn_setup():
        import jax, jax.numpy as jnp
        import numpy as np
        UNITS = 128
        NUM_HEADS = 16
        MASK_VALUE = -1000000000000.0

        def _split_heads(x, n):
            B, S, D = x.shape
            return x.reshape(B, S, n, D // n).transpose(0, 2, 1, 3)
        key = jax.random.key(seed)
        k1, k2, k3, k4 = jax.random.split(key, 4)
        B, S = (8, 128)
        memory = jax.random.normal(k1, (B, S, 2 * UNITS), dtype=jnp.float32)
        query = jax.random.normal(k2, (B, S, UNITS), dtype=jnp.float32)
        b = jax.random.normal(k3, (S,), dtype=jnp.float32)
        seq_len = jax.random.randint(k4, (B, 1), 0, S, dtype=jnp.int32)
        return {'memory': memory, 'query': query, 'b': b, 'seq_len': seq_len}
    _L0_xattn_all = _L0_xattn_setup()
    _L0_xattn_in = {k: v for k, v in _L0_xattn_all.items() if k in ('b',)}
    del _L0_xattn_all

    def _L0_ffn_setup():
        import jax, jax.numpy as jnp
        import numpy as np
        B, S, D_MODEL, D_FF, E, R, TOP_K = (4, 256, 128, 512, 8, 16, 2)
        key = jax.random.key(seed)
        ks = jax.random.split(key, 9)
        sd = 1.0 / np.sqrt(D_MODEL)
        return {'hidden_states': jax.random.normal(ks[0], (B, S, D_MODEL), jnp.float32), 'wi': jax.random.normal(ks[1], (D_FF, D_MODEL), jnp.float32) * sd, 'bi': jax.random.normal(ks[2], (D_FF,), jnp.float32) * 0.01, 'wo': jax.random.normal(ks[3], (D_MODEL, D_FF), jnp.float32) * (1.0 / np.sqrt(D_FF)), 'bo': jax.random.normal(ks[4], (D_MODEL,), jnp.float32) * 0.01, 'lora_A': jax.random.normal(ks[5], (E, R, D_MODEL), jnp.float32) * sd, 'lora_B': jax.random.normal(ks[6], (E, D_FF, R), jnp.float32) * 0.02, 'gate_w': jax.random.normal(ks[7], (E, D_MODEL), jnp.float32) * sd, 'gate_b': jax.random.normal(ks[8], (E,), jnp.float32) * 0.01}
    _L0_ffn_all = _L0_ffn_setup()
    _L0_ffn_in = {k: v for k, v in _L0_ffn_all.items() if k in ('wi', 'bi', 'wo', 'bo', 'lora_A', 'lora_B', 'gate_w', 'gate_b')}
    del _L0_ffn_all
    return {'x': x, 'ctx_2048': ctx_2048, 'itok_Bx1_68_817': itok_Bx1_68_817, 'g_xattn': g_xattn, 'g_ffn': g_ffn, 'L0_xattn_b': _L0_xattn_in['b'], 'L0_ffn_wi': _L0_ffn_in['wi'], 'L0_ffn_bi': _L0_ffn_in['bi'], 'L0_ffn_wo': _L0_ffn_in['wo'], 'L0_ffn_bo': _L0_ffn_in['bo'], 'L0_ffn_lora_A': _L0_ffn_in['lora_A'], 'L0_ffn_lora_B': _L0_ffn_in['lora_B'], 'L0_ffn_gate_w': _L0_ffn_in['gate_w'], 'L0_ffn_gate_b': _L0_ffn_in['gate_b']}

def reference(x, ctx_2048, itok_Bx1_68_817, g_xattn, g_ffn, L0_xattn_b, L0_ffn_wi, L0_ffn_bi, L0_ffn_wo, L0_ffn_bo, L0_ffn_lora_A, L0_ffn_lora_B, L0_ffn_gate_w, L0_ffn_gate_b):
    import jax
    import jax.numpy as jnp

    def _L0_xattn_ref(memory, query, b, seq_len):
        import jax, jax.numpy as jnp
        import numpy as np
        UNITS = 128
        NUM_HEADS = 16
        MASK_VALUE = -1000000000000.0

        def _split_heads(x, n):
            B, S, D = x.shape
            return x.reshape(B, S, n, D // n).transpose(0, 2, 1, 3)
        B, S, _ = query.shape
        dh = UNITS // NUM_HEADS
        k_mem, v_mem = jnp.split(memory, 2, axis=2)
        Q = _split_heads(query, NUM_HEADS) * dh ** (-0.5)
        Kh = _split_heads(k_mem, NUM_HEADS)
        Vh = _split_heads(v_mem, NUM_HEADS)
        logits = jnp.einsum('bhqd,bhkd->bhqk', Q, Kh) + b
        valid = (jnp.arange(S)[None, :] < seq_len[:, 0:1]).astype(jnp.float32)
        logits = logits + MASK_VALUE * (1.0 - valid)[:, None, None, :]
        weights = jax.nn.softmax(logits, axis=-1)
        out = jnp.einsum('bhqk,bhkd->bhqd', weights, Vh)
        return out.transpose(0, 2, 1, 3).reshape(B, S, UNITS)

    def _L0_ffn_ref(hidden_states, wi, bi, wo, bo, lora_A, lora_B, gate_w, gate_b):
        import jax, jax.numpy as jnp
        import numpy as np
        B, S, D_MODEL, D_FF, E, R, TOP_K = (4, 256, 128, 512, 8, 16, 2)
        logits = jnp.einsum('bsd,ed->bse', hidden_states, gate_w) + gate_b
        scores = jax.nn.softmax(logits, axis=-1)
        top_v, top_i = jax.lax.top_k(scores, TOP_K)
        val_sum = top_v.sum(axis=-1)
        out = jnp.zeros_like(hidden_states)
        for e in range(E):
            count = (top_i == e).sum(axis=-1).astype(hidden_states.dtype)
            gate = count * val_sum
            inter = jnp.einsum('bsd,fd->bsf', hidden_states, wi) + bi + jnp.einsum('bsr,fr->bsf', jnp.einsum('bsd,rd->bsr', hidden_states, lora_A[e]), lora_B[e])
            h = jax.nn.relu(inter)
            expert_out = jnp.einsum('bsf,df->bsd', h, wo) + bo
            out = out + gate[..., None] * expert_out
        return out
    x = x + jnp.tanh(g_xattn[0]) * _L0_xattn_ref(ctx_2048, _layernorm(x, axis=-1), L0_xattn_b, itok_Bx1_68_817)
    x = x + jnp.tanh(g_ffn[0]) * _L0_ffn_ref(_layernorm(x, axis=-1), L0_ffn_wi, L0_ffn_bi, L0_ffn_wo, L0_ffn_bo, L0_ffn_lora_A, L0_ffn_lora_B, L0_ffn_gate_w, L0_ffn_gate_b)
    return x

_drawn_inputs = setup_inputs


def setup_inputs(seed=0):
    import zlib

    import numpy as np

    out = dict(_drawn_inputs(seed))
    spreads = {}
    factors = {'L0_ffn_bi': 8.0, 'L0_ffn_bo': 6.976, 'L0_ffn_gate_b': 8.0}
    for name, (base, spread) in spreads.items():
        noise = np.random.default_rng([zlib.crc32(name.encode()), seed]).standard_normal(out[name].shape)
        drawn = base * np.exp(spread * noise) if base else spread * noise
        out[name] = jnp.asarray(drawn.astype(out[name].dtype))
    for name, factor in factors.items():
        out[name] = (out[name] * factor).astype(out[name].dtype)
    return out
```

```python
from contextlib import ExitStack

import concourse.bass as bass
from concourse import mybir

ALU = mybir.AluOpType
ACT = mybir.ActivationFunctionType
AX = mybir.AxisListType
F32 = mybir.dt.float32
BF16 = mybir.dt.bfloat16
I32 = mybir.dt.int32

MASK = -1.0e12
EPS = 1.0e-5

QPART = [0, 0, 1, 1, 0, 2]
KPART = [0, 1, 0, 1, 2, 0]
TERM_STEP = 15
BIAS_ROW = 120
MAX_ROW = 125
PARTS = 3


def flamingo(nc, x, ctx, seq_len, g_xattn, g_ffn, b, wi, bi, wo, bo, lora_a, lora_b, gate_w, gate_b, out):
    B, S, D = x.shape
    H = 16
    DH = D // H
    F = wi.shape[0]
    E, R, _ = lora_a.shape
    FC = F // 128
    PAIRS = B // 2
    SLOTS = 4
    CH = 4
    G = 4
    GT = 4
    GROUPS = B // GT
    UW = E * R + E
    STACK_ACT, STACK_SP = 5, 6

    es = ExitStack()
    with es:
        def sb(name, shape, dt):
            return es.enter_context(nc.sbuf_tensor(name, shape, dt))

        def psum(name, shape, dt):
            return es.enter_context(nc.psum_tensor(name, shape, dt))

        def sem(name):
            return es.enter_context(nc.semaphore(name))

        X = sb("X", [128, B, D], F32)
        V = sb("V", [128, B, D], F32)
        ident = sb("ident", [128, 128], F32)
        identb = sb("identb", [128, 128], BF16)
        onesf = sb("onesf", [128, 128], F32)
        onesb = sb("onesb", [128, 256], BF16)
        half_neg = sb("half_neg", [128, 4], F32)
        seq_row = sb("seq_row", [128, B], I32)
        qscale = sb("qscale", [128, B], F32)
        gates = sb("gates", [128, 2], F32)
        tanh_g = sb("tanh_g", [128, 2], F32)
        seq_col = sb("seq_col", [B, 1], I32)
        seq_colf = sb("seq_colf", [B, 1], F32)
        key_id = sb("key_id", [B, S], F32)
        b_rows = sb("b_rows", [B, S], F32)
        mask_rows = sb("mask_rows", [B, S], F32)
        bias_rows = sb("bias_rows", [B, S], F32)
        bias_rest = sb("bias_rest", [B, S], F32)
        bias_part = sb("bias_part", [B, PARTS, S], BF16)
        bias_line = sb("bias_line", [PARTS, B * S], BF16)
        kin = sb("kin", [128, SLOTS, 2, D], F32)
        stats = sb("stats", [128, 2, 6], F32)
        mv = sb("mv", [128, 2, 2], F32)
        veps = sb("veps", [128, 2, 2], F32)
        rstd = sb("rstd", [128, 2, 2], F32)
        qmul = sb("qmul", [128, 2, 2], F32)
        qadd = sb("qadd", [128, 2, 2], F32)
        xhat = sb("xhat", [128, 2, 2, D], F32)
        kperm = sb("kperm", [128, 2, 2, D], F32)
        full = sb("full", [128, 512], F32)
        rest = sb("rest", [128, 512], F32)
        part = [sb(f"part{i}", [128, 2, 512], BF16) for i in range(PARTS)]
        stack = sb("stack", [128, SLOTS, H, 512], BF16)
        negmax = sb("negmax", [128, 2, 2, H], F32)
        max_rest = sb("max_rest", [128, 2, H], F32)
        max_part = sb("max_part", [128, 2, 2, PARTS, H], BF16)
        max_rows = sb("max_rows", [PARTS * H, 2, 256], BF16)
        probs = sb("probs", [128, 3, 512], F32)
        vpad = sb("vpad", [128, 2, CH, G, 32], F32)
        o_rows = sb("o_rows", [128, 2, 256], F32)
        rsum = sb("rsum", [128, 2, CH, G], F32)
        o_norm = sb("o_norm", [128, 2, CH, G, DH], F32)
        wi_in = sb("wi_in", [128, FC, D], F32)
        wo_in = sb("wo_in", [128, F], F32)
        b_in = sb("b_in", [128, FC, E, R], F32)
        a_in = sb("a_in", [128, D], F32)
        gw_in = sb("gw_in", [E, D], F32)
        wiT = sb("wiT", [128, FC, 128], F32)
        woT = sb("woT", [128, FC, 128], F32)
        bT = sb("bT", [128, FC, 128], F32)
        agT = sb("agT", [128, UW], F32)
        bi_col = sb("bi_col", [128, FC], F32)
        nbi_col = sb("nbi_col", [128, FC], F32)
        bi_wide = sb("bi_wide", [128, FC, 128], F32)
        bo_rows = sb("bo_rows", [128, D], F32)
        shift = sb("shift", [128, D], F32)
        gb_rows = sb("gb_rows", [128, E], F32)
        first = sb("first", [128, E], F32)
        stats2 = sb("stats2", [128, GT, 6], F32)
        mv2 = sb("mv2", [128, GT, 2], F32)
        veps2 = sb("veps2", [128, GT], F32)
        rstd2 = sb("rstd2", [128, GT], F32)
        nmean2 = sb("nmean2", [128, GT], F32)
        xhat2 = sb("xhat2", [128, GT, D], F32)
        xT = sb("xT", [128, 2, 512], F32)
        lg = sb("lg", [128, GT, E], F32)
        lmax = sb("lmax", [128, GT], F32)
        lsh = sb("lsh", [128, GT, E], F32)
        lexp = sb("lexp", [128, GT, E], F32)
        lsum = sb("lsum", [128, GT], F32)
        score = sb("score", [128, GT, E], F32)
        top = sb("top", [128, 2, GT], F32)
        tie = sb("tie", [128, GT, E], F32)
        key = sb("key", [128, GT], F32)
        hot = sb("hot", [128, 2, GT, E], F32)
        hot_diff = sb("hot_diff", [128, GT, E], F32)
        gate = sb("gate", [128, 2, GT], F32)
        u = sb("u", [128, 2, GT, E, R], F32)
        uT = sb("uT", [128, 2, 2, 512], F32)
        h1 = sb("h1", [128, 2, 512], F32)
        hsum = sb("hsum", [128, FC, 512], F32)
        base = sb("base", [128, GT, D], F32)
        res = sb("res", [128, 2, GT, D], F32)

        bank = [psum(f"bank{i}", [128, 512], F32) for i in range(7)]
        bank_max = psum("bank_max", [128, 1024], BF16)
        sc1 = bank[0:2]
        sc2 = bank[2:4]
        o_acc, qk_t, o_t = bank[4:7]
        bank_out = bank_max[:, :].bitcast(F32)

        s_x = [sem(f"s_x{i}") for i in range(4)]
        s_v = [sem(f"s_v{i}") for i in range(4)]
        s_k = [sem(f"s_k{i}") for i in range(SLOTS)]
        s_small = sem("s_small")
        s_w = sem("s_w")
        s_pool_const = sem("s_pool_const")
        s_dve_const = sem("s_dve_const")
        s_bias = sem("s_bias")
        s_line = sem("s_line")
        s_zero = [sem(f"s_zero{i}") for i in range(SLOTS)]
        s_fixed = [sem(f"s_fixed{i}") for i in range(SLOTS)]
        s_tanh = sem("s_tanh")
        s_wT = sem("s_wT")
        s_wTc = sem("s_wTc")
        s_shift = sem("s_shift")
        s_stat = sem("s_stat")
        s_pow = sem("s_pow")
        s_kperm = sem("s_kperm")
        s_xhat = sem("s_xhat")
        s_qkT = sem("s_qkT")
        s_t1 = sem("s_t1")
        s_full = sem("s_full")
        s_rest = sem("s_rest")
        s_t2 = sem("s_t2")
        s_t3 = sem("s_t3")
        s_stack_act = [sem(f"s_stack_act{i}") for i in range(SLOTS)]
        s_stack_sp = [sem(f"s_stack_sp{i}") for i in range(SLOTS)]
        s_maxrow = [sem(f"s_maxrow{i}") for i in range(SLOTS)]
        s_sc1 = sem("s_sc1")
        s_max = sem("s_max")
        s_msplit = sem("s_msplit")
        s_mT = sem("s_mT")
        s_mTc = sem("s_mTc")
        s_sc2 = sem("s_sc2")
        s_exp = sem("s_exp")
        s_vpad = sem("s_vpad")
        s_pv = sem("s_pv")
        s_oc = sem("s_oc")
        s_oT = sem("s_oT")
        s_norm = sem("s_norm")
        s_stat2 = sem("s_stat2")
        s_pow2 = sem("s_pow2")
        s_xh2 = sem("s_xh2")
        s_xT = sem("s_xT")
        s_xTc = sem("s_xTc")
        s_ug = sem("s_ug")
        s_gate = sem("s_gate")
        s_gexp = sem("s_gexp")
        s_u = sem("s_u")
        s_uT = sem("s_uT")
        s_uTc = sem("s_uTc")
        s_a = sem("s_a")
        s_h1 = sem("s_h1")
        s_d = sem("s_d")
        s_hs = sem("s_hs")
        s_o = sem("s_o")
        s_fin = sem("s_fin")
        s_out = [sem("s_out0"), sem("s_out1")]

        NSTAT = 7
        NNORM = 5
        NMS = 4
        NST2 = 10
        NGATE = 21
        NFIN = 2 * GT
        POOL_CONSTS = 10

        def v_column(c):
            return (DH + 1) * c if c < CH - 1 else 0

        def chunk_bank(i):
            return bank[i % 3]

        def bank_cols(t):
            return t[:, :].rearrange("p (j k) -> p j k", j=G)

        block = es.enter_context(nc.Block())

        @block.sync
        def _(sp):
            ctx_t = ctx.rearrange("b s d -> s b d")
            x_t = x.rearrange("b s d -> s b d")

            def load_k(q):
                if q >= SLOTS:
                    sp.wait_ge(s_kperm, q - SLOTS + 1)
                sp.dma_start(kin[:, q % SLOTS, :, :], ctx_t[:, 2 * q:2 * q + 2, 0:D]).then_inc(s_k[q % SLOTS], 16)

            def load_x(i):
                n = B // 4
                sp.dma_start(X[:, n * i:n * i + n, :], x_t[:, n * i:n * i + n, :]).then_inc(s_x[i], 16)

            def load_v(i):
                n = B // 4
                sp.dma_start(V[:, n * i:n * i + n, :], ctx_t[:, n * i:n * i + n, D:2 * D]).then_inc(s_v[i], 16)

            load_x(0)
            load_k(0)
            load_k(1)
            load_k(2)
            load_k(3)
            load_v(0)
            def rows_of_ones(s):
                sp.wait_ge(s_zero[s], 1)
                sp.dma_start(stack[BIAS_ROW:BIAS_ROW + PARTS, s, :, 0:256],
                             onesb[0:PARTS, None, :].to_broadcast([PARTS, H, 256])).then_inc(s_fixed[s], 16)
                sp.dma_start(stack[MAX_ROW:MAX_ROW + PARTS, s, :, 256:512],
                             onesb[0:PARTS, None, :].to_broadcast([PARTS, H, 256])).then_inc(s_fixed[s], 16)

            sp.wait_ge(s_pool_const, 4)
            sp.wait_ge(s_bias, 6)
            for i in range(PARTS):
                sp.dma_start(bias_line[i:i + 1, :].rearrange("p (b k) -> p b k", b=B),
                             bias_part[:, i, :]).then_inc(s_line, 16)
            sp.wait_ge(s_line, 16 * PARTS)
            for i in range(1, 4):
                load_x(i)
                load_v(i)

            def stack_dmas(p):
                s, t = p % SLOTS, p % 2
                if p < SLOTS:
                    rows_of_ones(s)
                else:
                    sp.wait_ge(s_sc2, 2 * CH * (p - SLOTS + 1))
                dst = stack[:, s, :, :]
                inc = s_stack_sp[s]

                def rows(r, lo, hi):
                    return dst[r:r + TERM_STEP * (DH - 1) + 1:TERM_STEP, :, lo:hi]

                sp.dma_start(dst[BIAS_ROW:BIAS_ROW + PARTS, :, 256:512],
                             bias_line[:, None, 256 * p:256 * p + 256].to_broadcast([PARTS, H, 256])).then_inc(inc, 16)
                sp.wait_ge(s_t2, p + 1)
                sp.dma_start(rows(3, 0, 512), part[1][:, t, :]).then_inc(inc, 16)
                sp.dma_start(rows(2, 0, 256), part[1][:, t, 0:256]).then_inc(inc, 16)
                sp.dma_start(rows(1, 256, 512), part[1][:, t, 256:512]).then_inc(inc, 16)
                sp.wait_ge(s_t3, p + 1)
                sp.dma_start(rows(5, 0, 256), part[2][:, t, 0:256]).then_inc(inc, 16)
                sp.dma_start(rows(4, 256, 512), part[2][:, t, 256:512]).then_inc(inc, 16)

            for p in range(PAIRS):
                stack_dmas(p)
                if p + SLOTS < PAIRS:
                    load_k(p + SLOTS)

            for g in range(GROUPS):
                sp.wait_ge(s_fin, NFIN * (g + 1))
                sp.dma_start(out.rearrange("b s d -> s b d")[:, GT * g:GT * g + GT, :],
                             res[:, g % 2, :, :]).then_inc(s_out[g % 2], 16)
            sp.wait_ge(s_out[0], 16 * (GROUPS // 2))
            sp.wait_ge(s_out[1], 16 * (GROUPS // 2))

        @block.gpsimd
        def _(pool):
            pool.memset(ident[:, :], 0.0).then_inc(s_pool_const, 1)
            pool.memset(identb[:, :], 0.0).then_inc(s_pool_const, 1)
            pool.memset(onesf[:, :], 1.0).then_inc(s_pool_const, 1)
            pool.memset(onesb[:, :], 1.0).then_inc(s_pool_const, 1)
            pool.wait_ge(s_pool_const, 2)
            for m in (ident, identb):
                pool.affine_select(out=m[:, :], in_=m[:, :], compare_op=ALU.not_equal, fill=1.0, base=0,
                                   pattern=[[-1, 128]], channel_multiplier=1).then_inc(s_pool_const, 1)
            pool.memset(half_neg[:, :], -0.5).then_inc(s_pool_const, 1)
            pool.iota(key_id[:, :], pattern=[[1, S]], base=0, channel_multiplier=0,
                      allow_small_or_imprecise_dtypes=True).then_inc(s_pool_const, 1)
            pool.iota(first[:, :], pattern=[[-1, E]], base=E, channel_multiplier=0,
                      allow_small_or_imprecise_dtypes=True).then_inc(s_pool_const, 1)
            pool.memset(vpad[:, :, :, :, :], 0.0).then_inc(s_pool_const, 1)
            pool.wait_ge(s_pool_const, POOL_CONSTS)
            for s in range(2):
                for c in range(CH):
                    at = v_column(c) + DH
                    pool.memset(vpad[:, s, c, :, at:at + 1], 1.0).then_inc(s_vpad, 1)

            def perm(t):
                return t.rearrange("p b (h d) -> p b d h", h=H)

            def rsqrt(p):
                pool.wait_ge(s_stat, NSTAT * p + 5)
                pool.tensor_tensor(rstd[:, p % 2, :], veps[:, p % 2, :], half_neg[:, 0:2], ALU.pow).then_inc(s_pow, 1)

            def permute_k(p):
                pool.wait_ge(s_k[p % SLOTS], 16 * (p // SLOTS + 1))
                if p >= 2:
                    pool.wait_ge(s_qkT, p - 1)
                pool.tensor_copy(kperm[:, p % 2, :, :].rearrange("p b (d h) -> p b d h", h=H),
                                 perm(kin[:, p % SLOTS, :, :])).then_inc(s_kperm, 1)

            def normalise(p):
                pool.wait_ge(s_stat, NSTAT * (p + 1))
                if p >= 2:
                    pool.wait_ge(s_qkT, p - 1)
                for i in range(2):
                    pool.tensor_scalar(xhat[:, p % 2, i, :].rearrange("p (d h) -> p d h", h=H),
                                       X[:, 2 * p + i, :].rearrange("p (h d) -> p d h", h=H),
                                       qmul[:, p % 2, i:i + 1], qadd[:, p % 2, i:i + 1],
                                       ALU.mult, ALU.add).then_inc(s_xhat, 1)

            def place_v(n):
                if n % (B // 4) == 0:
                    pool.wait_ge(s_v[n // (B // 4)], 16)
                if n >= 2:
                    pool.wait_ge(s_pv, CH * (n - 1))
                else:
                    pool.wait_ge(s_vpad, 2 * CH)
                v = V[:, n, :].rearrange("p (c g d) -> p c g d", c=CH, g=G)
                for c in range(CH):
                    at = v_column(c)
                    pool.tensor_copy(vpad[:, n % 2, c, :, at:at + DH], v[:, c, :, :]).then_inc(s_vpad, 1)

            def remainders(p):
                pool.wait_ge(s_full, p + 1)
                if p >= 1:
                    pool.wait_ge(s_t2, p)
                    pool.wait_ge(s_t3, p)
                pool.tensor_tensor(rest[:, :], full[:, :], part[0][:, p % 2, :], ALU.subtract).then_inc(s_rest, 1)
                pool.wait_ge(s_t2, p + 1)
                pool.tensor_tensor(part[2][:, p % 2, :], rest[:, :], part[1][:, p % 2, :],
                                   ALU.subtract).then_inc(s_t3, 1)

            for q in range(-3, PAIRS + 3):
                if 0 <= q + 3 < PAIRS:
                    rsqrt(q + 3)
                if 0 <= 2 * q - 3 < B:
                    place_v(2 * q - 3)
                if 0 <= q + 3 < PAIRS:
                    permute_k(q + 3)
                    normalise(q + 3)
                if 0 <= 2 * q - 2 < B:
                    place_v(2 * q - 2)
                if 0 <= q + 2 < PAIRS:
                    remainders(q + 2)

            for g in range(GROUPS):
                pool.wait_ge(s_stat2, NST2 * g + 9)
                pool.tensor_tensor(rstd2[:, :], veps2[:, :], half_neg[:, :], ALU.pow).then_inc(s_pow2, 1)

        @block.scalar
        def _(act):
            act.dma_start(seq_row[:, :], seq_len.rearrange("b o -> o b").to_broadcast([128, B])).then_inc(s_small, 16)
            act.dma_start(seq_col[:, :], seq_len).then_inc(s_small, 16)
            act.dma_start(b_rows[:, :], b.rearrange("(o k) -> o k", o=1).to_broadcast([B, S])).then_inc(s_small, 16)
            act.dma_start(gates[:, 0:1], g_xattn.rearrange("(o k) -> o k", o=1).to_broadcast([128, 1])).then_inc(s_small, 16)
            act.dma_start(gates[:, 1:2], g_ffn.rearrange("(o k) -> o k", o=1).to_broadcast([128, 1])).then_inc(s_small, 16)
            act.dma_start(wi_in[:, :, :], wi.rearrange("(c p) d -> p c d", p=128)).then_inc(s_w, 16)
            act.dma_start(wo_in[:, :], wo).then_inc(s_w, 16)
            for c in range(FC):
                act.dma_start(b_in[:, c, :, :],
                              lora_b[:, c * 128:(c + 1) * 128, :].rearrange("e p r -> p e r")).then_inc(s_w, 16)
            act.dma_start(a_in[:, :], lora_a.rearrange("e r d -> (e r) d")).then_inc(s_w, 16)
            act.dma_start(gw_in[:, :], gate_w).then_inc(s_w, 16)
            with nc.allow_non_contiguous_dma(reason="512 biases to columns, once"):
                act.dma_start(bi_col[:, :], bi.rearrange("(c p) -> p c", p=128)).then_inc(s_w, 16)
            act.dma_start(bo_rows[:, :], bo.rearrange("(o k) -> o k", o=1).to_broadcast([128, D])).then_inc(s_w, 16)
            act.dma_start(gb_rows[:, :], gate_b.rearrange("(o k) -> o k", o=1).to_broadcast([128, E])).then_inc(s_w, 16)
            act.wait_ge(s_small, 80)
            act.activation(tanh_g[:, :], gates[:, :], ACT.Tanh).then_inc(s_tanh, 1)
            for i, (dst, src) in enumerate(((wiT[:, :, :].rearrange("p c f -> p (c f)"), sc2[0][:, :]),
                                            (woT[:, :, :].rearrange("p c f -> p (c f)"), sc2[1][:, :]),
                                            (bT[:, :, :].rearrange("p c f -> p (c f)"), o_acc[:, :]),
                                            (agT[:, :], o_t[:, 0:UW]))):
                act.wait_ge(s_wT, i + 1)
                act.activation(dst, src, ACT.Copy).then_inc(s_wTc, 1)

            def stack_dmas(p):
                s, t = p % SLOTS, p % 2
                if p < SLOTS:
                    act.wait_ge(s_zero[s], 1)
                else:
                    act.wait_ge(s_sc2, 2 * CH * (p - SLOTS + 1))
                act.wait_ge(s_t1, p + 1)
                inc = s_stack_act[s]

                def rows(r, lo, hi):
                    return stack[r:r + TERM_STEP * (DH - 1) + 1:TERM_STEP, s, :, lo:hi]

                act.dma_start(rows(0, 0, 512), part[0][:, t, :]).then_inc(inc, 16)
                act.dma_start(rows(1, 0, 256), part[0][:, t, 0:256]).then_inc(inc, 16)
                act.dma_start(rows(4, 0, 256), part[0][:, t, 0:256]).then_inc(inc, 16)
                act.dma_start(rows(2, 256, 512), part[0][:, t, 256:512]).then_inc(inc, 16)
                act.dma_start(rows(5, 256, 512), part[0][:, t, 256:512]).then_inc(inc, 16)

            def split(p):
                act.wait_ge(s_qkT, p + 1)
                if p >= 2:
                    o = (p - 2) % SLOTS
                    act.wait_ge(s_stack_act[o], 16 * STACK_ACT * ((p - 2) // SLOTS + 1))
                    act.wait_ge(s_stack_sp[o], 16 * STACK_SP * ((p - 2) // SLOTS + 1))
                act.activation(part[0][:, p % 2, :], qk_t[:, :], ACT.Copy).then_inc(s_t1, 1)
                if p >= 1:
                    act.wait_ge(s_rest, p)
                act.activation(full[:, :], qk_t[:, :], ACT.Copy).then_inc(s_full, 1)

            def second_part(p):
                act.wait_ge(s_rest, p + 1)
                act.activation(part[1][:, p % 2, :], rest[:, :], ACT.Copy).then_inc(s_t2, 1)

            def exps(n, c):
                i = CH * n + c
                act.wait_ge(s_sc2, i + 1)
                if i >= 3:
                    act.wait_ge(s_pv, i - 2)
                act.activation(probs[:, i % 3, :], sc2[i % 2][:, :], ACT.Exp).then_inc(s_exp, 1)

            def copy_o(n):
                act.wait_ge(s_pv, CH * (n + 1))
                if n >= 2:
                    act.wait_ge(s_oT, n - 1)
                act.activation(o_rows[:, n % 2, :], o_acc[:, 0:256], ACT.Copy).then_inc(s_oc, 1)

            def max_to_stack(p):
                act.wait_ge(s_mT, p + 1)
                if p >= 2:
                    act.wait_ge(s_maxrow[(p - 2) % SLOTS], 16 * ((p - 2) // SLOTS + 1))
                act.activation(max_rows[:, p % 2, :], bank_max[0:PARTS * H, 0:256], ACT.Copy).then_inc(s_mTc, 1)
                act.wait_ge(s_mTc, p + 1)
                act.dma_start(stack[MAX_ROW:MAX_ROW + PARTS, p % SLOTS, :, 0:256],
                              max_rows[:, p % 2, :]).then_inc(s_maxrow[p % SLOTS], 16)

            for q in range(-3, PAIRS + 3):
                if 0 <= q + 1 < PAIRS:
                    stack_dmas(q + 1)
                for i in range(2):
                    n = 2 * (q - 2) + i
                    for c in range(CH):
                        if 0 <= n < B:
                            exps(n, c)
                        if c == 0 and 0 <= n - 1 < B:
                            copy_o(n - 1)
                        if i == 0 and c == 2 and 0 <= q - 1 < PAIRS:
                            max_to_stack(q - 1)
                        if i == 1 and c == 1 and 0 <= q + 2 < PAIRS:
                            split(q + 2)
                if 0 <= q + 2 < PAIRS:
                    second_part(q + 2)

            def normalise(g):
                act.wait_ge(s_stat2, NST2 * (g + 1))
                act.wait_ge(s_pow2, g + 1)
                if g >= 1:
                    act.wait_ge(s_xT, g)
                for t in range(GT):
                    act.activation(xhat2[:, t, :], X[:, GT * g + t, :], ACT.Identity, bias=nmean2[:, t:t + 1],
                                   scale=rstd2[:, t:t + 1]).then_inc(s_xh2, 1)

            def copy_xT(g):
                act.wait_ge(s_xT, g + 1)
                if g >= 2:
                    act.wait_ge(s_d, FC * (g - 1))
                act.activation(xT[:, g % 2, :], qk_t[:, :], ACT.Copy).then_inc(s_xTc, 1)

            def gate_exp(g):
                act.wait_ge(s_gate, NGATE * g + 4)
                act.activation(lexp[:, :, :], lsh[:, :, :], ACT.Exp).then_inc(s_gexp, 1)

            def copy_uT(g):
                for i, src in enumerate((qk_t, o_t)):
                    act.wait_ge(s_uT, 2 * g + i + 1)
                    if g >= 2:
                        act.wait_ge(s_d, FC * (g - 1))
                    act.activation(uT[:, g % 2, i, :], src[:, :], ACT.Copy).then_inc(s_uTc, 1)

            def relu(g, c):
                i = FC * g + c
                act.wait_ge(s_a, i + 1)
                if i >= 2:
                    act.wait_ge(s_hs, i - 1)
                act.activation(h1[:, i % 2, :], chunk_bank(i)[:, :], ACT.Relu,
                               bias=bi_col[:, c:c + 1]).then_inc(s_h1, 1)

            for g in range(-2, GROUPS):
                if 0 <= g + 1 < GROUPS:
                    copy_xT(g + 1)
                if g >= 0:
                    relu(g, 0)
                    relu(g, 1)
                if 0 <= g + 1 < GROUPS:
                    gate_exp(g + 1)
                if g >= 0:
                    relu(g, 2)
                    relu(g, 3)
                if 0 <= g + 2 < GROUPS:
                    normalise(g + 2)
                if 0 <= g + 1 < GROUPS:
                    copy_uT(g + 1)

        @block.tensor
        def _(pe):
            pe.wait_ge(s_pool_const, 6)
            pe.wait_ge(s_w, 16 * 11)
            for c in range(FC):
                mm = pe.transpose(sc2[0][:, c * 128:(c + 1) * 128], wi_in[:, c, :], ident[:, :])
            mm.then_inc(s_wT, 1)
            for c in range(FC):
                mm = pe.transpose(sc2[1][:, c * 128:(c + 1) * 128], wo_in[:, c * 128:(c + 1) * 128], ident[:, :])
            mm.then_inc(s_wT, 1)
            for c in range(FC):
                mm = pe.transpose(o_acc[:, c * 128:(c + 1) * 128],
                                  b_in[:, c, :, :].rearrange("p e r -> p (e r)"), ident[:, :])
            mm.then_inc(s_wT, 1)
            pe.transpose(o_t[:, 0:128], a_in[:, :], ident[:, :])
            pe.transpose(o_t[:, 128:UW], gw_in[:, :], ident[0:E, 0:E]).then_inc(s_wT, 1)
            pe.wait_ge(s_wTc, 2)
            pe.wait_ge(s_shift, 2)
            for c in range(FC):
                mm = pe.matmul(qk_t[:, 0:D], bi_wide[:, c, :], woT[:, c, :], start=(c == 0), stop=(c == FC - 1))
            mm.then_inc(s_wT, 1)

            def transpose_qk(p):
                pe.wait_ge(s_xhat, 2 * (p + 1))
                pe.wait_ge(s_kperm, p + 1)
                if p == 0:
                    pe.wait_ge(s_shift, 3)
                else:
                    pe.wait_ge(s_full, p)
                for i in range(2):
                    pe.transpose(qk_t[:, i * 128:(i + 1) * 128], xhat[:, p % 2, i, :], ident[:, :])
                for i in range(2):
                    mm = pe.transpose(qk_t[:, 256 + i * 128:256 + (i + 1) * 128], kperm[:, p % 2, i, :], ident[:, :])
                mm.then_inc(s_qkT, 1)

            def pass1(n, c):
                i, p, s = CH * n + c, n // 2, (n // 2) % SLOTS
                if c == 0 and n % 2 == 0:
                    pe.wait_ge(s_stack_act[s], 16 * STACK_ACT * (p // SLOTS + 1))
                    pe.wait_ge(s_stack_sp[s], 16 * STACK_SP * (p // SLOTS + 1))
                    if p < SLOTS:
                        pe.wait_ge(s_fixed[s], 32)
                if i >= 2:
                    pe.wait_ge(s_max, i - 1)
                q0 = (n % 2) * 128
                for j in range(G):
                    h = c * G + j
                    mm = pe.matmul(sc1[i % 2][:, j * 128:(j + 1) * 128], stack[0:MAX_ROW, s, h, q0:q0 + 128],
                                   stack[0:MAX_ROW, s, h, 256 + q0:384 + q0], start=True, stop=True)
                mm.then_inc(s_sc1, 1)

            def transpose_max(p):
                pe.wait_ge(s_msplit, NMS * (p + 1))
                if p >= 1:
                    pe.wait_ge(s_mTc, p)
                for i in range(2):
                    mm = pe.transpose(bank_max[0:PARTS * H, i * 128:(i + 1) * 128],
                                      max_part[:, p % 2, i, :, :].rearrange("p t h -> p (t h)"), identb[:, :])
                mm.then_inc(s_mT, 1)

            def pass2(n, c):
                i, p, s = CH * n + c, n // 2, (n // 2) % SLOTS
                if c == 0 and n % 2 == 0:
                    pe.wait_ge(s_maxrow[s], 16 * (p // SLOTS + 1))
                if i == 0:
                    pe.wait_ge(s_wTc, 4)
                if i >= 2:
                    pe.wait_ge(s_exp, i - 1)
                q0 = (n % 2) * 128
                for j in range(G):
                    h = c * G + j
                    mm = pe.matmul(sc2[i % 2][:, j * 128:(j + 1) * 128], stack[:, s, h, 256 + q0:384 + q0],
                                   stack[:, s, h, q0:q0 + 128], start=True, stop=True)
                mm.then_inc(s_sc2, 1)

            def weigh_v(n, c):
                i = CH * n + c
                if c == 0:
                    pe.wait_ge(s_vpad, 2 * CH + CH * (n + 1))
                    if n >= 1:
                        pe.wait_ge(s_oc, n)
                pe.wait_ge(s_exp, i + 1)
                c0 = 128 if c == CH - 1 else 0
                for j in range(G):
                    mm = pe.matmul(o_acc[32 * j:32 * j + 32, c0:c0 + 128], vpad[:, n % 2, c, j, :],
                                   probs[:, i % 3, j * 128:(j + 1) * 128], start=(c in (0, CH - 1)),
                                   stop=(c >= CH - 2))
                mm.then_inc(s_pv, 1)

            def transpose_o(n):
                pe.wait_ge(s_oc, n + 1)
                if n >= 1:
                    pe.wait_ge(s_norm, NNORM * (n - 1) + 4)
                for i in range(2):
                    mm = pe.transpose(o_t[:, i * 128:(i + 1) * 128], o_rows[:, n % 2, i * 128:(i + 1) * 128], ident[:, :])
                mm.then_inc(s_oT, 1)

            for q in range(-3, PAIRS + 3):
                for i in range(2):
                    m, n = 2 * q + i, 2 * (q - 2) + i
                    if i == 1 and 0 <= q + 2 < PAIRS:
                        transpose_qk(q + 2)
                    for c in range(CH):
                        if 0 <= m < B:
                            pass1(m, c)
                        if 0 <= n < B:
                            pass2(n, c)
                        if c == 2 and 0 <= n - 1 < B:
                            transpose_o(n - 1)
                        if c > 0 and 0 <= n < B:
                            weigh_v(n, c - 1)
                        if i == 0 and c == 1 and 0 <= q - 1 < PAIRS:
                            transpose_max(q - 1)
                    if 0 <= n < B:
                        weigh_v(n, CH - 1)

            def transpose_x(g):
                pe.wait_ge(s_xh2, GT * (g + 1))
                if g >= 1:
                    pe.wait_ge(s_uTc, 2 * g)
                for t in range(GT):
                    mm = pe.transpose(qk_t[:, t * 128:(t + 1) * 128], xhat2[:, t, :], ident[:, :])
                mm.then_inc(s_xT, 1)

            def lora_and_gates(g):
                pe.wait_ge(s_xTc, g + 1)
                if g >= 1:
                    pe.wait_ge(s_u, 4 * g)
                for t in range(GT):
                    c0 = (t % 2) * UW
                    mm = pe.matmul(bank[3 + t // 2][:, c0:c0 + UW], xT[:, g % 2, t * 128:(t + 1) * 128], agT[:, :],
                                   start=True, stop=True)
                mm.then_inc(s_ug, 1)

            def transpose_u(g):
                for i, dst in enumerate((qk_t, o_t)):
                    pe.wait_ge(s_u, 4 * g + 2 * (i + 1))
                    if i == 0:
                        pe.wait_ge(s_xTc, g + 1)
                    elif g >= 1:
                        pe.wait_ge(s_uTc, 2 * g)
                    for t in range(GT):
                        mm = pe.transpose(dst[:, t * 128:(t + 1) * 128],
                                          u[:, i, t, :, :].rearrange("p e r -> p (e r)"), ident[:, :])
                    mm.then_inc(s_uT, 1)

            def first_expert(g, c):
                i = FC * g + c
                if c == 0:
                    pe.wait_ge(s_uTc, 2 * (g + 1))
                if i >= 3:
                    pe.wait_ge(s_hs, i - 2)
                pe.matmul(chunk_bank(i)[:, :], wiT[:, c, :], xT[:, g % 2, :], start=True, stop=False)
                pe.matmul(chunk_bank(i)[:, :], bT[:, c, :], uT[:, g % 2, 0, :], start=False,
                          stop=True).then_inc(s_a, 1)

            def second_expert(g, c):
                i = FC * g + c
                pe.wait_ge(s_h1, i + 1)
                pe.matmul(chunk_bank(i)[:, :], bT[:, c, :], uT[:, g % 2, 1, :], start=False, stop=True,
                          skip_group_check=True).then_inc(s_d, 1)

            def out_weights(g):
                pe.wait_ge(s_hs, FC * (g + 1))
                if g >= 1:
                    pe.wait_ge(s_fin, NFIN * g)
                for t in range(GT):
                    for c in range(FC):
                        mm = pe.matmul(bank_out[:, t * 128:(t + 1) * 128], hsum[:, c, t * 128:(t + 1) * 128], woT[:, c, :],
                                       start=(c == 0), stop=(c == FC - 1))
                mm.then_inc(s_o, 1)

            pe.wait_ge(s_norm, NNORM * B)
            for g in range(-1, GROUPS):
                if g + 1 < GROUPS:
                    transpose_x(g + 1)
                if g >= 0:
                    first_expert(g, 0)
                    first_expert(g, 1)
                if g + 1 < GROUPS:
                    lora_and_gates(g + 1)
                if g >= 0:
                    second_expert(g, 0)
                    first_expert(g, 2)
                    second_expert(g, 1)
                    first_expert(g, 3)
                    second_expert(g, 2)
                    second_expert(g, 3)
                if g + 1 < GROUPS:
                    transpose_u(g + 1)
                if g >= 0:
                    out_weights(g)

        @block.vector
        def _(dve):
            U32 = mybir.dt.uint32
            words = stack[:, :, :, :].bitcast(U32)
            dve.memset(words[:, 0, :, :], 0).then_inc(s_zero[0], 1)

            dve.wait_ge(s_small, 80)
            dve.tensor_scalar(qscale[:, :], seq_row[:, :], 0.0, float(DH) ** -0.5, ALU.is_gt,
                              ALU.mult).then_inc(s_dve_const, 1)
            dve.tensor_copy(seq_colf[:, :], seq_col[:, :]).then_inc(s_bias, 1)
            dve.wait_ge(s_pool_const, 8)
            dve.wait_ge(s_bias, 1)
            dve.tensor_scalar(mask_rows[:, :], key_id[:, :], seq_colf[:, 0:1], MASK, ALU.is_ge,
                              ALU.mult).then_inc(s_bias, 1)
            dve.wait_ge(s_bias, 2)
            dve.tensor_tensor(bias_rows[:, :], mask_rows[:, :], b_rows[:, :], ALU.add).then_inc(s_bias, 1)
            dve.wait_ge(s_bias, 3)
            dve.tensor_copy(bias_part[:, 0, :], bias_rows[:, :]).then_inc(s_bias, 1)
            dve.wait_ge(s_bias, 4)
            dve.tensor_tensor(bias_rest[:, :], bias_rows[:, :], bias_part[:, 0, :], ALU.subtract).then_inc(s_bias, 1)
            dve.wait_ge(s_bias, 5)
            dve.tensor_copy(bias_part[:, 1, :], bias_rest[:, :]).then_inc(s_dve_const, 1)
            dve.wait_ge(s_dve_const, 2)
            dve.tensor_tensor(bias_part[:, 2, :], bias_rest[:, :], bias_part[:, 1, :], ALU.subtract).then_inc(s_bias, 1)

            def stats1(p):
                o = NSTAT * p
                if p % (PAIRS // 4) == 0:
                    dve.wait_ge(s_x[p // (PAIRS // 4)], 16)
                for i in range(2):
                    dve.bn_stats(stats[:, i, :], X[:, 2 * p + i, :]).then_inc(s_stat, 1)
                for i in range(2):
                    dve.wait_ge(s_stat, o + i + 1)
                    dve.bn_aggr(mv[:, i, :], stats[:, i, :]).then_inc(s_stat, 1)
                dve.wait_ge(s_stat, o + 4)
                if p >= 2:
                    dve.wait_ge(s_pow, p - 1)
                dve.tensor_scalar(veps[:, p % 2, :], mv[:, :, 1], EPS, None, ALU.add).then_inc(s_stat, 1)

            def scales1(p):
                o = NSTAT * p
                dve.wait_ge(s_pow, p + 1)
                if p >= 2:
                    dve.wait_ge(s_xhat, 2 * (p - 1))
                if p == 0:
                    dve.wait_ge(s_dve_const, 1)
                dve.tensor_tensor(qmul[:, p % 2, :], rstd[:, p % 2, :], qscale[:, 2 * p:2 * p + 2],
                                  ALU.mult).then_inc(s_stat, 1)
                dve.wait_ge(s_stat, o + 6)
                dve.scalar_tensor_tensor(out=qadd[:, p % 2, :], in0=mv[:, :, 0], scalar=-1.0, in1=qmul[:, p % 2, :],
                                         op0=ALU.mult, op1=ALU.mult).then_inc(s_stat, 1)

            def row_max(n, c):
                i, p = CH * n + c, n // 2
                dve.wait_ge(s_sc1, i + 1)
                dve.tensor_reduce(negmax[:, p % 2, n % 2, c * G:(c + 1) * G], bank_cols(sc1[i % 2]), AX.X, ALU.max,
                                  negate=True).then_inc(s_max, 1)

            def split_max(p):
                o = NMS * p
                dve.wait_ge(s_max, 2 * CH * (p + 1))
                if p >= 2:
                    dve.wait_ge(s_mT, p - 1)
                src = negmax[:, p % 2, :, :]
                dst = max_part[:, p % 2, :, :, :]
                dve.tensor_copy(dst[:, :, 0, :], src).then_inc(s_msplit, 1)
                dve.wait_ge(s_msplit, o + 1)
                dve.tensor_tensor(max_rest[:, :, :], src, dst[:, :, 0, :], ALU.subtract).then_inc(s_msplit, 1)
                dve.wait_ge(s_msplit, o + 2)
                dve.tensor_copy(dst[:, :, 1, :], max_rest[:, :, :]).then_inc(s_msplit, 1)
                dve.wait_ge(s_msplit, o + 3)
                dve.tensor_tensor(dst[:, :, 2, :], max_rest[:, :, :], dst[:, :, 1, :],
                                  ALU.subtract).then_inc(s_msplit, 1)

            def add_attention(n):
                o = NNORM * n
                C3 = CH - 1
                if n == 0:
                    dve.wait_ge(s_tanh, 1)
                dve.wait_ge(s_oT, n + 1)
                a = o_t[:, 0:128].rearrange("p (g w) -> p g w", g=G)
                z = o_t[:, 128:256].rearrange("p (g w) -> p g w", g=G)
                sums = a[:, :, 0:9 * C3].rearrange("p g (c w) -> p c g w", c=C3)
                rs = rsum[:, n % 2, :, :]
                on = o_norm[:, n % 2, :, :, :]
                dve.reciprocal(rs[:, 0:C3, :], sums[:, :, :, DH]).then_inc(s_norm, 1)
                dve.reciprocal(rs[:, C3, :], z[:, :, DH]).then_inc(s_norm, 1)
                dve.wait_ge(s_norm, o + 2)
                dve.tensor_tensor(on[:, 0:C3, :, :], sums[:, :, :, 0:DH],
                                  rs[:, 0:C3, :, None].to_broadcast([128, C3, G, DH]), ALU.mult).then_inc(s_norm, 1)
                dve.tensor_tensor(on[:, C3, :, :], z[:, :, 0:DH],
                                  rs[:, C3, :, None].to_broadcast([128, G, DH]), ALU.mult).then_inc(s_norm, 1)
                dve.wait_ge(s_norm, o + 4)
                dve.scalar_tensor_tensor(out=X[:, n, :], in0=on.rearrange("p c g d -> p (c g d)"),
                                         scalar=tanh_g[:, 0:1], in1=X[:, n, :], op0=ALU.mult,
                                         op1=ALU.add).then_inc(s_norm, 1)

            for q in range(-3, PAIRS + 3):
                if 0 <= q + 3 < PAIRS:
                    stats1(q + 3)
                if q == -3:
                    for s in range(1, SLOTS):
                        dve.memset(words[:, s, :, :], 0).then_inc(s_zero[s], 1)
                for i in range(2):
                    m, n = 2 * q + i, 2 * (q - 2) + i
                    for c in range(CH):
                        if 0 <= m < B:
                            row_max(m, c)
                        if c == 2 and 0 <= n - 1 < B:
                            add_attention(n - 1)
                    if i == 0 and 0 <= q + 3 < PAIRS:
                        scales1(q + 3)
                    if q == -2 and i == 0:
                        dve.wait_ge(s_w, 16 * 11)
                        dve.wait_ge(s_pool_const, 3)
                        dve.tensor_scalar(nbi_col[:, :], bi_col[:, :], -1.0, None, ALU.mult).then_inc(s_shift, 1)
                        dve.tensor_copy(bi_wide[:, :, :],
                                        bi_col[:, :, None].to_broadcast([128, FC, 128])).then_inc(s_shift, 1)
                    if q == -2 and i == 1:
                        dve.wait_ge(s_wT, 5)
                        dve.scalar_tensor_tensor(out=shift[:, :], in0=bo_rows[:, :], scalar=2.0, in1=qk_t[:, 0:D],
                                                 op0=ALU.mult, op1=ALU.add).then_inc(s_shift, 1)
                if 0 <= q < PAIRS:
                    split_max(q)

            def stats2_of(g):
                o = NST2 * g
                if g >= 1:
                    dve.wait_ge(s_xh2, GT * g)
                for t in range(GT):
                    dve.bn_stats(stats2[:, t, :], X[:, GT * g + t, :]).then_inc(s_stat2, 1)
                for t in range(GT):
                    dve.wait_ge(s_stat2, o + t + 1)
                    dve.bn_aggr(mv2[:, t, :], stats2[:, t, :]).then_inc(s_stat2, 1)
                dve.wait_ge(s_stat2, o + 8)
                dve.tensor_scalar(veps2[:, :], mv2[:, :, 1], EPS, None, ALU.add).then_inc(s_stat2, 1)

            def shifts2(g):
                dve.wait_ge(s_pow2, g + 1)
                dve.scalar_tensor_tensor(out=nmean2[:, :], in0=mv2[:, :, 0], scalar=-1.0, in1=rstd2[:, :],
                                         op0=ALU.mult, op1=ALU.mult).then_inc(s_stat2, 1)

            def wide(t):
                return t[:, :, None].to_broadcast([128, GT, E])

            steps = [0]

            def gate_step(ins):
                steps[0] += 1
                ins.then_inc(s_gate, 1)

            def last_step():
                dve.wait_ge(s_gate, steps[0])

            def gates_shift(g):
                dve.wait_ge(s_ug, g + 1)
                for i in range(2):
                    src = bank[3 + i][:, 0:2 * UW].rearrange("p (t w) -> p t w", t=2)[:, :, E * R:UW]
                    gate_step(dve.tensor_tensor(lg[:, 2 * i:2 * i + 2, :], src,
                                                gb_rows[:, None, :].to_broadcast([128, 2, E]), ALU.add))
                last_step()
                gate_step(dve.tensor_reduce(lmax[:, :], lg[:, :, :], AX.X, ALU.max))
                last_step()
                if g >= 1:
                    dve.wait_ge(s_gexp, g)
                gate_step(dve.tensor_tensor(lsh[:, :, :], lg[:, :, :], wide(lmax), ALU.subtract))

            def gates_pick(g):
                dve.wait_ge(s_gexp, g + 1)
                gate_step(dve.tensor_reduce(lsum[:, :], lexp[:, :, :], AX.X, ALU.add))
                last_step()
                gate_step(dve.reciprocal(lmax[:, :], lsum[:, :]))
                last_step()
                gate_step(dve.tensor_tensor(score[:, :, :], lexp[:, :, :], wide(lmax), ALU.mult))
                for i in range(2):
                    last_step()
                    gate_step(dve.tensor_reduce(top[:, i, :], score[:, :, :], AX.X, ALU.max))
                    last_step()
                    gate_step(dve.tensor_tensor(tie[:, :, :], score[:, :, :], wide(top[:, i, :]), ALU.is_equal))
                    last_step()
                    gate_step(dve.tensor_tensor(lg[:, :, :], tie[:, :, :],
                                                first[:, None, :].to_broadcast([128, GT, E]), ALU.mult))
                    last_step()
                    gate_step(dve.tensor_reduce(key[:, :], lg[:, :, :], AX.X, ALU.max))
                    last_step()
                    gate_step(dve.tensor_tensor(hot[:, i, :, :], lg[:, :, :], wide(key), ALU.is_equal))
                    if i == 0:
                        last_step()
                        gate_step(dve.scalar_tensor_tensor(
                            out=score[:, :, :].rearrange("p t e -> p (t e)"),
                            in0=hot[:, 0, :, :].rearrange("p t e -> p (t e)"), scalar=-2.0,
                            in1=score[:, :, :].rearrange("p t e -> p (t e)"), op0=ALU.mult, op1=ALU.add))
                gate_step(dve.tensor_tensor(lsum[:, :], top[:, 0, :], top[:, 1, :], ALU.add))
                last_step()
                gate_step(dve.tensor_tensor(hot_diff[:, :, :], hot[:, 1, :, :], hot[:, 0, :, :], ALU.subtract))
                gate_step(dve.tensor_scalar(gate[:, g % 2, :], lsum[:, :], tanh_g[:, 1:2], None, ALU.mult))

            def mask_u(g):
                last_step()
                if g >= 1:
                    dve.wait_ge(s_uT, 2 * g)
                for k, m in enumerate((hot[:, 0, :, :], hot_diff[:, :, :])):
                    for i in range(2):
                        for_tiles = bank[3 + i][:, 0:2 * UW].rearrange("p (t w) -> p t w", t=2)[:, :, 0:E * R]
                        dve.tensor_tensor(u[:, k, 2 * i:2 * i + 2, :, :],
                                          for_tiles.rearrange("p t (e r) -> p t e r", e=E),
                                          m[:, 2 * i:2 * i + 2, :, None].to_broadcast([128, 2, E, R]),
                                          ALU.mult).then_inc(s_u, 1)

            def sum_experts(g, c):
                i = FC * g + c
                dve.wait_ge(s_d, i + 1)
                dve.scalar_tensor_tensor(out=hsum[:, c, :], in0=chunk_bank(i)[:, :], scalar=nbi_col[:, c:c + 1],
                                         in1=h1[:, i % 2, :], op0=ALU.max, op1=ALU.add).then_inc(s_hs, 1)

            def finish(g):
                o = NFIN * g
                if g >= 2:
                    dve.wait_ge(s_out[g % 2], 16 * (g // 2))
                for t in range(GT):
                    dve.scalar_tensor_tensor(out=base[:, t, :], in0=shift[:, :], scalar=gate[:, g % 2, t:t + 1],
                                             in1=X[:, GT * g + t, :], op0=ALU.mult, op1=ALU.add).then_inc(s_fin, 1)
                dve.wait_ge(s_o, g + 1)
                for t in range(GT):
                    dve.wait_ge(s_fin, o + t + 1)
                    dve.scalar_tensor_tensor(out=res[:, g % 2, t, :], in0=bank_out[:, t * 128:(t + 1) * 128],
                                             scalar=gate[:, g % 2, t:t + 1], in1=base[:, t, :], op0=ALU.mult,
                                             op1=ALU.add).then_inc(s_fin, 1)

            dve.wait_ge(s_norm, NNORM * B)
            for g in range(-2, GROUPS):
                if g + 2 < GROUPS:
                    stats2_of(g + 2)
                if 0 <= g + 1 < GROUPS:
                    gates_shift(g + 1)
                if g >= 0:
                    sum_experts(g, 0)
                if 0 <= g + 1 < GROUPS:
                    gates_pick(g + 1)
                if g + 2 < GROUPS:
                    shifts2(g + 2)
                if g >= 0:
                    sum_experts(g, 1)
                if 0 <= g + 1 < GROUPS:
                    mask_u(g + 1)
                if g >= 0:
                    sum_experts(g, 2)
                    sum_experts(g, 3)
                    finish(g)


_INS = ["x", "ctx_2048", "itok_Bx1_68_817", "g_xattn", "g_ffn", "L0_xattn_b", "L0_ffn_wi", "L0_ffn_bi", "L0_ffn_wo",
        "L0_ffn_bo", "L0_ffn_lora_A", "L0_ffn_lora_B", "L0_ffn_gate_w", "L0_ffn_gate_b"]


def kernel(**inputs):
    import numpy as _np
    import concourse.bacc as _bacc
    from concourse import mybir as _mybir
    from concourse.bass_utils import run_bass_kernel_spmd as _run

    nc = _bacc.Bacc("TRN2", target_bir_lowering=False, num_devices=1)
    arrays, args = {}, []
    for name in _INS:
        a = _np.ascontiguousarray(inputs[name])
        arrays[f"in_{name}_dram"] = a
        args.append(nc.dram_tensor(f"in_{name}_dram", a.shape, _mybir.dt.from_np(a.dtype), kind="ExternalInput").ap())
    shape = inputs["x"].shape
    args.append(nc.dram_tensor("out_0_dram", shape, _mybir.dt.float32, kind="ExternalOutput").ap())
    flamingo(nc, *args)
    r = _run(nc, [arrays], core_ids=[0])
    return r.results[0]["out_0_dram"]
```

```python
from contextlib import ExitStack

import concourse.bass as bass
from concourse import mybir

ALU = mybir.AluOpType
ACT = mybir.ActivationFunctionType
AX = mybir.AxisListType
F32 = mybir.dt.float32
BF16 = mybir.dt.bfloat16
I32 = mybir.dt.int32

MASK = -1.0e12
EPS = 1.0e-5

QPART = [0, 0, 1, 1, 0, 2]
KPART = [0, 1, 0, 1, 2, 0]
TERM_STEP = 15
BIAS_ROW = 120
MAX_ROW = 125
PARTS = 3


def flamingo(nc, x, ctx, seq_len, g_xattn, g_ffn, b, wi, bi, wo, bo, lora_a, lora_b, gate_w, gate_b, out):
    B, S, D = x.shape
    H = 16
    DH = D // H
    F = wi.shape[0]
    E, R, _ = lora_a.shape
    FC = F // 128
    PAIRS = B // 2
    QUADS = B // 4
    SLOTS = 3
    CH = 4
    G = 4
    GT = 4
    GROUPS = B // GT
    UW = E * R + E
    STACK_DMAS = 11

    es = ExitStack()
    with es:
        def sb(name, shape, dt):
            return es.enter_context(nc.sbuf_tensor(name, shape, dt))

        def psum(name, shape, dt):
            return es.enter_context(nc.psum_tensor(name, shape, dt))

        def sem(name):
            return es.enter_context(nc.semaphore(name))

        X = sb("X", [128, B, D], F32)
        V = sb("V", [128, B, D], F32)
        ident = sb("ident", [128, 128], F32)
        identb = sb("identb", [128, 128], BF16)
        onesf = sb("onesf", [128, 128], F32)
        onesb = sb("onesb", [128, 512], BF16)
        zeros = sb("zeros", [128, 1], F32)
        half_neg = sb("half_neg", [128, 4], F32)
        seq_row = sb("seq_row", [128, B], I32)
        qscale = sb("qscale", [128, B], F32)
        gates = sb("gates", [128, 2], F32)
        tanh_g = sb("tanh_g", [128, 2], F32)
        seq_col = sb("seq_col", [B, 1], I32)
        seq_colf = sb("seq_colf", [B, 1], F32)
        key_id = sb("key_id", [B, S], F32)
        b_rows = sb("b_rows", [B, S], F32)
        mask_rows = sb("mask_rows", [B, S], F32)
        bias_rows = sb("bias_rows", [B, S], F32)
        bias_rest = sb("bias_rest", [B, S], F32)
        bias_part = sb("bias_part", [B, PARTS, S], BF16)
        bias_line = sb("bias_line", [PARTS, B * S], BF16)
        kin = sb("kin", [128, 2, 4, D], F32)
        stats = sb("stats", [128, 2, 6], F32)
        mv = sb("mv", [128, 2, 2], F32)
        veps = sb("veps", [128, 2, 2], F32)
        rstd = sb("rstd", [128, 2, 2], F32)
        qmul = sb("qmul", [128, 2, 2], F32)
        qadd = sb("qadd", [128, 2, 2], F32)
        xhat = sb("xhat", [128, 2, 2, D], F32)
        kperm = sb("kperm", [128, 2, 2, D], F32)
        full = sb("full", [128, 512], F32)
        rest = sb("rest", [128, 512], F32)
        part = [sb(f"part{i}", [128, 2, 2, 512], BF16) for i in range(PARTS)]
        stack = sb("stack", [128, SLOTS, H, 1024], BF16)
        negmax = sb("negmax", [128, 2, 2, H], F32)
        max_rest = sb("max_rest", [128, 2, H], F32)
        max_part = sb("max_part", [128, 2, 2, PARTS, H], BF16)
        max_rows = sb("max_rows", [PARTS * H, 2, 256], BF16)
        probs = sb("probs", [128, 3, 512], F32)
        vpad = sb("vpad", [128, 2, CH * 137], F32)
        o_rows = sb("o_rows", [128, 2, 256], F32)
        rsum = sb("rsum", [128, 2, CH, G], F32)
        o_norm = sb("o_norm", [128, 2, CH, G, DH], F32)
        wi_in = sb("wi_in", [128, FC, D], F32)
        wo_in = sb("wo_in", [128, F], F32)
        b_in = sb("b_in", [128, FC, E, R], F32)
        a_in = sb("a_in", [128, D], F32)
        gw_in = sb("gw_in", [E, D], F32)
        wiT = sb("wiT", [128, FC, 128], F32)
        woT = sb("woT", [128, FC, 128], F32)
        bT = sb("bT", [128, FC, 128], F32)
        agT = sb("agT", [128, UW], F32)
        bi_col = sb("bi_col", [128, FC], F32)
        nbi_col = sb("nbi_col", [128, FC], F32)
        bi_wide = sb("bi_wide", [128, FC, 128], F32)
        bo_rows = sb("bo_rows", [128, D], F32)
        shift = sb("shift", [128, D], F32)
        gb_rows = sb("gb_rows", [128, E], F32)
        first = sb("first", [128, E], F32)
        stats2 = sb("stats2", [128, GT, 6], F32)
        mv2 = sb("mv2", [128, GT, 2], F32)
        veps2 = sb("veps2", [128, GT], F32)
        rstd2 = sb("rstd2", [128, GT], F32)
        nmean2 = sb("nmean2", [128, GT], F32)
        lg = sb("lg", [128, GT, E], F32)
        lmax = sb("lmax", [128, GT], F32)
        lsh = sb("lsh", [128, GT, E], F32)
        lexp = sb("lexp", [128, GT, E], F32)
        lsum = sb("lsum", [128, GT], F32)
        score = sb("score", [128, GT, E], F32)
        top = sb("top", [128, 2, GT], F32)
        tie = sb("tie", [128, GT, E], F32)
        key = sb("key", [128, GT], F32)
        hot = sb("hot", [128, 2, GT, E], F32)
        hot_diff = sb("hot_diff", [128, GT, E], F32)
        gate = sb("gate", [128, 2, GT], F32)

        bank = [psum(f"bank{i}", [128, 512], F32) for i in range(7)]
        bank_max = psum("bank_max", [128, 1024], BF16)
        sc1 = bank[0:2]
        sc2 = bank[2:4]
        o_acc, qk_t, o_t = bank[4:7]
        bank_out = bank_max[:, :].bitcast(F32)

        s_x = [sem(f"s_x{i}") for i in range(QUADS)]
        s_v = [sem(f"s_v{i}") for i in range(QUADS)]
        s_k = [sem(f"s_k{i}") for i in range(2)]
        s_small = sem("s_small")
        s_w = sem("s_w")
        s_pool_const = sem("s_pool_const")
        s_dve_const = sem("s_dve_const")
        s_bias = sem("s_bias")
        s_line = sem("s_line")
        s_zero = [sem(f"s_zero{i}") for i in range(SLOTS)]
        s_fixed = [sem(f"s_fixed{i}") for i in range(SLOTS)]
        s_tanh = sem("s_tanh")
        s_wT = sem("s_wT")
        s_wTc = sem("s_wTc")
        s_shift = sem("s_shift")
        s_stat = sem("s_stat")
        s_pow = sem("s_pow")
        s_kperm = sem("s_kperm")
        s_xhat = sem("s_xhat")
        s_qkT = sem("s_qkT")
        s_t1 = sem("s_t1")
        s_full = sem("s_full")
        s_rest = sem("s_rest")
        s_t2 = sem("s_t2")
        s_t3 = sem("s_t3")
        s_stack = [sem(f"s_stack{i}") for i in range(SLOTS)]
        s_maxrow = [sem(f"s_maxrow{i}") for i in range(4)]
        s_sc1 = sem("s_sc1")
        s_max = sem("s_max")
        s_msplit = sem("s_msplit")
        s_mT = sem("s_mT")
        s_mTc = sem("s_mTc")
        s_sc2 = sem("s_sc2")
        s_exp = sem("s_exp")
        s_vpad = sem("s_vpad")
        s_pv = sem("s_pv")
        s_oc = sem("s_oc")
        s_oT = sem("s_oT")
        s_norm = sem("s_norm")
        s_stat2 = sem("s_stat2")
        s_pow2 = sem("s_pow2")
        s_xh2 = sem("s_xh2")
        s_xT = sem("s_xT")
        s_xTc = sem("s_xTc")
        s_ug = sem("s_ug")
        s_gate = sem("s_gate")
        s_gexp = sem("s_gexp")
        s_u = sem("s_u")
        s_uT = sem("s_uT")
        s_uTc = sem("s_uTc")
        s_a = sem("s_a")
        s_h1 = sem("s_h1")
        s_d = sem("s_d")
        s_hs = sem("s_hs")
        s_o = sem("s_o")
        s_fin = sem("s_fin")
        s_out = [sem("s_out0"), sem("s_out1")]

        NSTAT = 7
        NNORM = 5
        NMS = 4
        NST2 = 10
        NGATE = 21
        NFIN = 2 * GT
        POOL_CONSTS = 11

        words = stack[:, :, :, :].bitcast(F32)

        def reuse(slot, row, rows):
            return words[:, slot, row:row + rows, :]

        xhat2 = reuse(2, 0, 1).rearrange("p o (t d) -> p (o t) d", t=GT)
        xT = reuse(2, 1, 2)
        u = reuse(2, 3, 2).rearrange("p k (t e r) -> p k t e r", t=GT, e=E)
        uT = reuse(2, 5, 4).rearrange("p (s k) c -> p s k c", s=2)
        h1 = reuse(2, 9, 2)
        hsum = reuse(2, 11, FC)
        base = reuse(0, 0, 1).rearrange("p o (t d) -> p (o t) d", t=GT)
        res = reuse(0, 1, 2).rearrange("p s (t d) -> p s t d", t=GT)

        def pair_cols(t, p):
            return t[:, (p // 2) % 2, :, 256 * (p % 2):256 * (p % 2) + 256]

        def halves(t):
            return t[:, :].rearrange("p (s c) -> p s c", s=2)

        def v_window(n, c, g):
            at = (c * G + g) * 32
            return vpad[:, n % 2, at:at + 32]

        def v_column(c):
            return (DH + 1) * c if c < CH - 1 else 0

        def chunk_bank(i):
            return bank[i % 3]

        def bank_cols(t):
            return t[:, :].rearrange("p (j k) -> p j k", j=G)

        block = es.enter_context(nc.Block())

        @block.sync
        def _(sp):
            ctx_t = ctx.rearrange("b s d -> s b d")
            x_t = x.rearrange("b s d -> s b d")

            def load_k(Q):
                if Q >= 2:
                    sp.wait_ge(s_kperm, 2 * (Q - 1))
                sp.dma_start(kin[:, Q % 2, :, :], ctx_t[:, 4 * Q:4 * Q + 4, 0:D]).then_inc(s_k[Q % 2], 16)

            def load_x(Q):
                sp.dma_start(X[:, 4 * Q:4 * Q + 4, :], x_t[:, 4 * Q:4 * Q + 4, :]).then_inc(s_x[Q], 16)

            def load_v(Q):
                sp.dma_start(V[:, 4 * Q:4 * Q + 4, :], ctx_t[:, 4 * Q:4 * Q + 4, D:2 * D]).then_inc(s_v[Q], 16)

            def rows_of_ones(s):
                sp.wait_ge(s_zero[s], 2)
                sp.dma_start(stack[BIAS_ROW:BIAS_ROW + PARTS, s, :, 0:512],
                             onesb[0:PARTS, None, :].to_broadcast([PARTS, H, 512])).then_inc(s_fixed[s], 16)
                sp.dma_start(stack[MAX_ROW:MAX_ROW + PARTS, s, :, 512:1024],
                             onesb[0:PARTS, None, :].to_broadcast([PARTS, H, 512])).then_inc(s_fixed[s], 16)

            def stack_dmas(Q):
                s, t = Q % SLOTS, Q % 2
                if Q >= SLOTS:
                    sp.wait_ge(s_sc2, 4 * CH * (Q - SLOTS + 1))
                inc = s_stack[s]

                def rows(r, lo, hi):
                    return stack[r:r + TERM_STEP * (DH - 1) + 1:TERM_STEP, s, :, lo:hi]

                sp.dma_start(stack[BIAS_ROW:BIAS_ROW + PARTS, s, :, 512:1024],
                             bias_line[:, None, 512 * Q:512 * Q + 512].to_broadcast([PARTS, H, 512])).then_inc(inc, 16)
                for i, ready in enumerate((s_t1, s_t2, s_t3)):
                    sp.wait_ge(ready, 2 * (Q + 1))
                    for r in range(len(QPART)):
                        if QPART[r] == i and KPART[r] == i:
                            sp.dma_start(rows(r, 0, 1024), part[i][:, t, :, :].rearrange("p s c -> p (s c)")).then_inc(inc, 16)
                        elif QPART[r] == i:
                            sp.dma_start(rows(r, 0, 512), part[i][:, t, 0, :]).then_inc(inc, 16)
                        elif KPART[r] == i:
                            sp.dma_start(rows(r, 512, 1024), part[i][:, t, 1, :]).then_inc(inc, 16)

            def max_to_stack(p):
                sp.wait_ge(s_mTc, p + 1)
                c0 = 256 * (p % 2)
                sp.dma_start(stack[MAX_ROW:MAX_ROW + PARTS, (p // 2) % SLOTS, :, c0:c0 + 256],
                             max_rows[:, p % 2, :]).then_inc(s_maxrow[p % 4], 16)

            def load_weights():
                sp.dma_start(wi_in[:, :, :], wi.rearrange("(c p) d -> p c d", p=128)).then_inc(s_w, 16)
                sp.dma_start(wo_in[:, :], wo).then_inc(s_w, 16)
                for c in range(FC):
                    sp.dma_start(b_in[:, c, :, :],
                                 lora_b[:, c * 128:(c + 1) * 128, :].rearrange("e p r -> p e r")).then_inc(s_w, 16)
                sp.dma_start(a_in[:, :], lora_a.rearrange("e r d -> (e r) d")).then_inc(s_w, 16)
                sp.dma_start(gw_in[:, :], gate_w).then_inc(s_w, 16)
                with nc.allow_non_contiguous_dma(reason="512 biases to columns, once"):
                    sp.dma_start(bi_col[:, :], bi.rearrange("(c p) -> p c", p=128)).then_inc(s_w, 16)
                sp.dma_start(bo_rows[:, :], bo.rearrange("(o k) -> o k", o=1).to_broadcast([128, D])).then_inc(s_w, 16)
                sp.dma_start(gb_rows[:, :], gate_b.rearrange("(o k) -> o k", o=1).to_broadcast([128, E])).then_inc(s_w, 16)

            load_x(0)
            load_k(0)
            load_x(1)
            load_k(1)
            sp.wait_ge(s_bias, 6)
            for i in range(PARTS):
                sp.dma_start(bias_line[i:i + 1, :].rearrange("p (b k) -> p b k", b=B),
                             bias_part[:, i, :]).then_inc(s_line, 16)
            sp.wait_ge(s_pool_const, 4)
            rows_of_ones(0)
            sp.wait_ge(s_line, 16 * PARTS)
            stack_dmas(0)
            load_v(0)
            rows_of_ones(1)
            load_x(2)
            rows_of_ones(2)

            for q in range(PAIRS + 1):
                if q % 2 == 1 and q // 2 + 1 < QUADS:
                    stack_dmas(q // 2 + 1)
                if q >= 1:
                    max_to_stack(q - 1)
                if q % 2 == 0 and q // 2 < QUADS:
                    if q // 2 + 2 < QUADS:
                        load_k(q // 2 + 2)
                    if q // 2 + 3 < QUADS:
                        load_x(q // 2 + 3)
                    if q // 2 + 1 < QUADS:
                        load_v(q // 2 + 1)
                if q == 8:
                    load_weights()

            for g in range(GROUPS):
                sp.wait_ge(s_fin, NFIN * (g + 1))
                sp.dma_start(out.rearrange("b s d -> s b d")[:, GT * g:GT * g + GT, :],
                             res[:, g % 2, :, :]).then_inc(s_out[g % 2], 16)
            sp.wait_ge(s_out[0], 16 * (GROUPS // 2))
            sp.wait_ge(s_out[1], 16 * (GROUPS // 2))

        @block.gpsimd
        def _(pool):
            pool.memset(ident[:, :], 0.0).then_inc(s_pool_const, 1)
            pool.memset(identb[:, :], 0.0).then_inc(s_pool_const, 1)
            pool.memset(onesf[:, :], 1.0).then_inc(s_pool_const, 1)
            pool.memset(onesb[:, :], 1.0).then_inc(s_pool_const, 1)
            pool.wait_ge(s_pool_const, 2)
            for m in (ident, identb):
                pool.affine_select(out=m[:, :], in_=m[:, :], compare_op=ALU.not_equal, fill=1.0, base=0,
                                   pattern=[[-1, 128]], channel_multiplier=1).then_inc(s_pool_const, 1)
            pool.memset(half_neg[:, :], -0.5).then_inc(s_pool_const, 1)
            pool.iota(key_id[:, :], pattern=[[1, S]], base=0, channel_multiplier=0,
                      allow_small_or_imprecise_dtypes=True).then_inc(s_pool_const, 1)
            pool.memset(zeros[:, :], 0.0).then_inc(s_pool_const, 1)
            pool.iota(first[:, :], pattern=[[-1, E]], base=E, channel_multiplier=0,
                      allow_small_or_imprecise_dtypes=True).then_inc(s_pool_const, 1)
            pool.memset(vpad[:, :, :], 0.0).then_inc(s_pool_const, 1)
            pool.wait_ge(s_pool_const, POOL_CONSTS)
            for s in range(2):
                for c in range(CH):
                    for g in range(G):
                        at = (c * G + g) * 32 + v_column(c) + DH
                        last = pool.memset(vpad[:, s, at:at + 1], 1.0)
                    last.then_inc(s_vpad, 1)

            def perm(t):
                return t.rearrange("p b (h d) -> p b d h", h=H)

            def rsqrt(p):
                pool.wait_ge(s_stat, NSTAT * p + 5)
                pool.tensor_tensor(rstd[:, p % 2, :], veps[:, p % 2, :], half_neg[:, 0:2], ALU.pow).then_inc(s_pow, 1)

            def permute_k(p):
                pool.wait_ge(s_k[(p // 2) % 2], 16 * (p // 4 + 1))
                if p >= 2:
                    pool.wait_ge(s_qkT, p - 1)
                pool.tensor_copy(kperm[:, p % 2, :, :].rearrange("p b (d h) -> p b d h", h=H),
                                 perm(kin[:, (p // 2) % 2, 2 * (p % 2):2 * (p % 2) + 2, :])).then_inc(s_kperm, 1)

            def normalise(p):
                pool.wait_ge(s_stat, NSTAT * (p + 1))
                if p >= 2:
                    pool.wait_ge(s_qkT, p - 1)
                for i in range(2):
                    pool.tensor_scalar(xhat[:, p % 2, i, :].rearrange("p (d h) -> p d h", h=H),
                                       X[:, 2 * p + i, :].rearrange("p (h d) -> p d h", h=H),
                                       qmul[:, p % 2, i:i + 1], qadd[:, p % 2, i:i + 1],
                                       ALU.mult, ALU.add).then_inc(s_xhat, 1)

            def place_v(n):
                if n % 4 == 0:
                    pool.wait_ge(s_v[n // 4], 16)
                if n >= 2:
                    pool.wait_ge(s_pv, CH * (n - 1))
                else:
                    pool.wait_ge(s_vpad, 2 * CH)
                v = V[:, n, :].rearrange("p (c g d) -> p c g d", c=CH, g=G)
                dst = vpad[:, n % 2, :].rearrange("p (c w) -> p c w", c=CH)[:, 0:CH - 1, 0:128]
                pool.tensor_copy(dst.rearrange("p c (g w) -> p c g w", g=G)[:, :, :, 0:DH],
                                 v[:, 0:CH - 1, :, :]).then_inc(s_vpad, 1)
                dst = vpad[:, n % 2, 128 * (CH - 1):128 * CH].rearrange("p (g w) -> p g w", g=G)
                pool.tensor_copy(dst[:, :, 0:DH], v[:, CH - 1, :, :]).then_inc(s_vpad, 1)

            def remainders(p):
                pool.wait_ge(s_full, p + 1)
                if p >= 1:
                    pool.wait_ge(s_t2, p)
                    pool.wait_ge(s_t3, p)
                pool.tensor_tensor(halves(rest), halves(full), pair_cols(part[0], p), ALU.subtract).then_inc(s_rest, 1)
                pool.wait_ge(s_t2, p + 1)
                pool.tensor_tensor(pair_cols(part[2], p), halves(rest), pair_cols(part[1], p),
                                   ALU.subtract).then_inc(s_t3, 1)

            for q in range(-4, PAIRS + 3):
                if 0 <= q + 4 < PAIRS:
                    rsqrt(q + 4)
                if 0 <= 2 * q - 3 < B:
                    place_v(2 * q - 3)
                if 0 <= q + 4 < PAIRS:
                    permute_k(q + 4)
                    normalise(q + 4)
                if 0 <= 2 * q - 2 < B:
                    place_v(2 * q - 2)
                if 0 <= q + 3 < PAIRS:
                    remainders(q + 3)

            for g in range(GROUPS):
                pool.wait_ge(s_stat2, NST2 * g + 9)
                pool.tensor_tensor(rstd2[:, :], veps2[:, :], half_neg[:, :], ALU.pow).then_inc(s_pow2, 1)

        @block.scalar
        def _(act):
            act.dma_start(seq_row[:, :], seq_len.rearrange("b o -> o b").to_broadcast([128, B])).then_inc(s_small, 16)
            act.dma_start(seq_col[:, :], seq_len).then_inc(s_small, 16)
            act.dma_start(b_rows[:, :], b.rearrange("(o k) -> o k", o=1).to_broadcast([B, S])).then_inc(s_small, 16)
            act.dma_start(gates[:, 0:1], g_xattn.rearrange("(o k) -> o k", o=1).to_broadcast([128, 1])).then_inc(s_small, 16)
            act.dma_start(gates[:, 1:2], g_ffn.rearrange("(o k) -> o k", o=1).to_broadcast([128, 1])).then_inc(s_small, 16)
            act.wait_ge(s_small, 80)
            act.activation(tanh_g[:, :], gates[:, :], ACT.Tanh).then_inc(s_tanh, 1)

            def zero_half(s):
                half = words[:, s, H // 2:H, :]
                act.activation(half, zeros[:, 0:1, None].to_broadcast([128, H // 2, 512]), ACT.Copy).then_inc(s_zero[s], 1)

            def copy_weights(i):
                dst = (wiT, woT, bT)[i][:, :, :].rearrange("p c f -> p (c f)") if i < 3 else agT[:, :]
                act.wait_ge(s_wT, i + 1)
                act.activation(dst, qk_t[:, 0:dst.shape[1]], ACT.Copy).then_inc(s_wTc, 1)

            def split(p):
                act.wait_ge(s_qkT, p + 1)
                if p >= 4:
                    old = p // 2 - 2
                    act.wait_ge(s_stack[old % SLOTS], 16 * STACK_DMAS * (old // SLOTS + 1))
                act.activation(pair_cols(part[0], p), halves(qk_t), ACT.Copy).then_inc(s_t1, 1)
                if p >= 1:
                    act.wait_ge(s_rest, p)
                act.activation(full[:, :], qk_t[:, :], ACT.Copy).then_inc(s_full, 1)

            def second_part(p):
                act.wait_ge(s_rest, p + 1)
                act.activation(pair_cols(part[1], p), halves(rest), ACT.Copy).then_inc(s_t2, 1)

            def exps(n, c):
                i = CH * n + c
                act.wait_ge(s_sc2, i + 1)
                if i >= 3:
                    act.wait_ge(s_pv, i - 2)
                act.activation(probs[:, i % 3, :], sc2[i % 2][:, :], ACT.Exp).then_inc(s_exp, 1)

            def copy_o(n):
                act.wait_ge(s_pv, CH * (n + 1))
                if n >= 2:
                    act.wait_ge(s_oT, n - 1)
                act.activation(o_rows[:, n % 2, :], o_acc[:, 0:256], ACT.Copy).then_inc(s_oc, 1)

            def copy_max(p):
                act.wait_ge(s_mT, p + 1)
                if p >= 2:
                    act.wait_ge(s_maxrow[(p - 2) % 4], 16 * ((p - 2) // 4 + 1))
                act.activation(max_rows[:, p % 2, :], bank_max[0:PARTS * H, 0:256], ACT.Copy).then_inc(s_mTc, 1)

            act.wait_ge(s_pool_const, POOL_CONSTS)
            zero_half(0)
            for q in range(-4, PAIRS + 3):
                for i in range(2):
                    n = 2 * (q - 2) + i
                    for c in range(CH):
                        if 0 <= n < B:
                            exps(n, c)
                        if c == 0 and 0 <= n - 1 < B:
                            copy_o(n - 1)
                        if i == 0 and c == 2 and 0 <= q - 1 < PAIRS:
                            copy_max(q - 1)
                        if i == 1 and c == 1 and 0 <= q + 3 < PAIRS:
                            split(q + 3)
                        if i == 1 and c == 1 and 0 <= q - (PAIRS - 3) < 4:
                            copy_weights(q - (PAIRS - 3))
                if 0 <= q + 3 < PAIRS:
                    second_part(q + 3)
                if q in (-3, -2):
                    zero_half(q + 4)

            def normalise(g):
                act.wait_ge(s_stat2, NST2 * (g + 1))
                act.wait_ge(s_pow2, g + 1)
                if g >= 1:
                    act.wait_ge(s_xT, g)
                for t in range(GT):
                    act.activation(xhat2[:, t, :], X[:, GT * g + t, :], ACT.Identity, bias=nmean2[:, t:t + 1],
                                   scale=rstd2[:, t:t + 1]).then_inc(s_xh2, 1)

            def copy_xT(g):
                act.wait_ge(s_xT, g + 1)
                if g >= 2:
                    act.wait_ge(s_d, FC * (g - 1))
                act.activation(xT[:, g % 2, :], qk_t[:, :], ACT.Copy).then_inc(s_xTc, 1)

            def gate_exp(g):
                act.wait_ge(s_gate, NGATE * g + 4)
                act.activation(lexp[:, :, :], lsh[:, :, :], ACT.Exp).then_inc(s_gexp, 1)

            def copy_uT(g):
                for i, src in enumerate((qk_t, o_t)):
                    act.wait_ge(s_uT, 2 * g + i + 1)
                    if g >= 2:
                        act.wait_ge(s_d, FC * (g - 1))
                    act.activation(uT[:, g % 2, i, :], src[:, :], ACT.Copy).then_inc(s_uTc, 1)

            def relu(g, c):
                i = FC * g + c
                act.wait_ge(s_a, i + 1)
                if i >= 2:
                    act.wait_ge(s_hs, i - 1)
                act.activation(h1[:, i % 2, :], chunk_bank(i)[:, :], ACT.Relu,
                               bias=bi_col[:, c:c + 1]).then_inc(s_h1, 1)

            for g in range(-2, GROUPS):
                if 0 <= g + 1 < GROUPS:
                    copy_xT(g + 1)
                if g >= 0:
                    relu(g, 0)
                    relu(g, 1)
                if 0 <= g + 1 < GROUPS:
                    gate_exp(g + 1)
                if g >= 0:
                    relu(g, 2)
                    relu(g, 3)
                if 0 <= g + 2 < GROUPS:
                    normalise(g + 2)
                if 0 <= g + 1 < GROUPS:
                    copy_uT(g + 1)

        @block.tensor
        def _(pe):
            pe.wait_ge(s_pool_const, 6)

            def transpose_weights(k):
                if k == 0:
                    pe.wait_ge(s_w, 16 * 11)
                    pe.wait_ge(s_full, PAIRS)
                else:
                    pe.wait_ge(s_wTc, k)
                if k == 3:
                    pe.transpose(qk_t[:, 0:128], a_in[:, :], ident[:, :])
                    mm = pe.transpose(qk_t[:, 128:UW], gw_in[:, :], ident[0:E, 0:E])
                elif k == 4:
                    pe.wait_ge(s_shift, 2)
                    for c in range(FC):
                        mm = pe.matmul(qk_t[:, 0:D], bi_wide[:, c, :], woT[:, c, :], start=(c == 0), stop=(c == FC - 1))
                else:
                    for c in range(FC):
                        src = (wi_in[:, c, :], wo_in[:, c * 128:(c + 1) * 128],
                               b_in[:, c, :, :].rearrange("p e r -> p (e r)"))[k]
                        mm = pe.transpose(qk_t[:, c * 128:(c + 1) * 128], src, ident[:, :])
                mm.then_inc(s_wT, 1)

            def transpose_qk(p):
                pe.wait_ge(s_xhat, 2 * (p + 1))
                pe.wait_ge(s_kperm, p + 1)
                if p >= 1:
                    pe.wait_ge(s_full, p)
                for i in range(2):
                    pe.transpose(qk_t[:, i * 128:(i + 1) * 128], xhat[:, p % 2, i, :], ident[:, :])
                for i in range(2):
                    mm = pe.transpose(qk_t[:, 256 + i * 128:256 + (i + 1) * 128], kperm[:, p % 2, i, :], ident[:, :])
                mm.then_inc(s_qkT, 1)

            def pass1(n, c):
                i, Q, s = CH * n + c, n // 4, (n // 4) % SLOTS
                if c == 0 and n % 4 == 0:
                    pe.wait_ge(s_stack[s], 16 * STACK_DMAS * (Q // SLOTS + 1))
                    if Q < SLOTS:
                        pe.wait_ge(s_fixed[s], 32)
                if i >= 2:
                    pe.wait_ge(s_max, i - 1)
                q0 = (n % 4) * 128
                for j in range(G):
                    h = c * G + j
                    mm = pe.matmul(sc1[i % 2][:, j * 128:(j + 1) * 128], stack[0:MAX_ROW, s, h, q0:q0 + 128],
                                   stack[0:MAX_ROW, s, h, 512 + q0:640 + q0], start=True, stop=True)
                mm.then_inc(s_sc1, 1)

            def transpose_max(p):
                pe.wait_ge(s_msplit, NMS * (p + 1))
                if p >= 1:
                    pe.wait_ge(s_mTc, p)
                for i in range(2):
                    mm = pe.transpose(bank_max[0:PARTS * H, i * 128:(i + 1) * 128],
                                      max_part[:, p % 2, i, :, :].rearrange("p t h -> p (t h)"), identb[:, :])
                mm.then_inc(s_mT, 1)

            def pass2(n, c):
                i, p, s = CH * n + c, n // 2, (n // 4) % SLOTS
                if c == 0 and n % 2 == 0:
                    pe.wait_ge(s_maxrow[p % 4], 16 * (p // 4 + 1))
                if i >= 2:
                    pe.wait_ge(s_exp, i - 1)
                q0 = (n % 4) * 128
                for j in range(G):
                    h = c * G + j
                    mm = pe.matmul(sc2[i % 2][:, j * 128:(j + 1) * 128], stack[:, s, h, 512 + q0:640 + q0],
                                   stack[:, s, h, q0:q0 + 128], start=True, stop=True)
                mm.then_inc(s_sc2, 1)

            def weigh_v(n, c):
                i = CH * n + c
                if c == 0:
                    pe.wait_ge(s_vpad, 2 * CH + 2 * (n + 1))
                    if n >= 1:
                        pe.wait_ge(s_oc, n)
                pe.wait_ge(s_exp, i + 1)
                c0 = 128 if c == CH - 1 else 0
                for j in range(G):
                    mm = pe.matmul(o_acc[32 * j:32 * j + 32, c0:c0 + 128], v_window(n, c, j),
                                   probs[:, i % 3, j * 128:(j + 1) * 128], start=(c in (0, CH - 1)),
                                   stop=(c >= CH - 2))
                mm.then_inc(s_pv, 1)

            def transpose_o(n):
                pe.wait_ge(s_oc, n + 1)
                if n >= 1:
                    pe.wait_ge(s_norm, NNORM * (n - 1) + 4)
                for i in range(2):
                    mm = pe.transpose(o_t[:, i * 128:(i + 1) * 128], o_rows[:, n % 2, i * 128:(i + 1) * 128], ident[:, :])
                mm.then_inc(s_oT, 1)

            for q in range(-4, PAIRS + 3):
                for i in range(2):
                    m, n = 2 * q + i, 2 * (q - 2) + i
                    if i == 1 and 0 <= q + 3 < PAIRS:
                        transpose_qk(q + 3)
                    if i == 1 and 0 <= q - (PAIRS - 3) < 5:
                        transpose_weights(q - (PAIRS - 3))
                    for c in range(CH):
                        if 0 <= m < B:
                            pass1(m, c)
                        if 0 <= n < B:
                            pass2(n, c)
                        if c == 2 and 0 <= n - 1 < B:
                            transpose_o(n - 1)
                        if c > 0 and 0 <= n < B:
                            weigh_v(n, c - 1)
                        if i == 0 and c == 1 and 0 <= q - 1 < PAIRS:
                            transpose_max(q - 1)
                    if 0 <= n < B:
                        weigh_v(n, CH - 1)

            def transpose_x(g):
                pe.wait_ge(s_xh2, GT * (g + 1))
                if g >= 1:
                    pe.wait_ge(s_uTc, 2 * g)
                for t in range(GT):
                    mm = pe.transpose(qk_t[:, t * 128:(t + 1) * 128], xhat2[:, t, :], ident[:, :])
                mm.then_inc(s_xT, 1)

            def lora_and_gates(g):
                pe.wait_ge(s_xTc, g + 1)
                if g >= 1:
                    pe.wait_ge(s_u, 4 * g)
                for t in range(GT):
                    c0 = (t % 2) * UW
                    mm = pe.matmul(bank[3 + t // 2][:, c0:c0 + UW], xT[:, g % 2, t * 128:(t + 1) * 128], agT[:, :],
                                   start=True, stop=True)
                mm.then_inc(s_ug, 1)

            def transpose_u(g):
                for i, dst in enumerate((qk_t, o_t)):
                    pe.wait_ge(s_u, 4 * g + 2 * (i + 1))
                    if i == 0:
                        pe.wait_ge(s_xTc, g + 1)
                    elif g >= 1:
                        pe.wait_ge(s_uTc, 2 * g)
                    for t in range(GT):
                        mm = pe.transpose(dst[:, t * 128:(t + 1) * 128],
                                          u[:, i, t, :, :].rearrange("p e r -> p (e r)"), ident[:, :])
                    mm.then_inc(s_uT, 1)

            def first_expert(g, c):
                i = FC * g + c
                if c == 0:
                    pe.wait_ge(s_uTc, 2 * (g + 1))
                if i >= 3:
                    pe.wait_ge(s_hs, i - 2)
                pe.matmul(chunk_bank(i)[:, :], wiT[:, c, :], xT[:, g % 2, :], start=True, stop=False)
                pe.matmul(chunk_bank(i)[:, :], bT[:, c, :], uT[:, g % 2, 0, :], start=False,
                          stop=True).then_inc(s_a, 1)

            def second_expert(g, c):
                i = FC * g + c
                pe.wait_ge(s_h1, i + 1)
                pe.matmul(chunk_bank(i)[:, :], bT[:, c, :], uT[:, g % 2, 1, :], start=False, stop=True,
                          skip_group_check=True).then_inc(s_d, 1)

            def out_weights(g):
                pe.wait_ge(s_hs, FC * (g + 1))
                if g >= 1:
                    pe.wait_ge(s_fin, NFIN * g)
                for t in range(GT):
                    for c in range(FC):
                        mm = pe.matmul(bank_out[:, t * 128:(t + 1) * 128], hsum[:, c, t * 128:(t + 1) * 128], woT[:, c, :],
                                       start=(c == 0), stop=(c == FC - 1))
                mm.then_inc(s_o, 1)

            pe.wait_ge(s_norm, NNORM * B)
            pe.wait_ge(s_shift, 3)
            for g in range(-1, GROUPS):
                if g + 1 < GROUPS:
                    transpose_x(g + 1)
                if g >= 0:
                    first_expert(g, 0)
                    first_expert(g, 1)
                if g + 1 < GROUPS:
                    lora_and_gates(g + 1)
                if g >= 0:
                    second_expert(g, 0)
                    first_expert(g, 2)
                    second_expert(g, 1)
                    first_expert(g, 3)
                    second_expert(g, 2)
                    second_expert(g, 3)
                if g + 1 < GROUPS:
                    transpose_u(g + 1)
                if g >= 0:
                    out_weights(g)

        @block.vector
        def _(dve):
            def zero_half(s):
                dve.memset(words[:, s, 0:H // 2, :], 0.0).then_inc(s_zero[s], 1)

            zero_half(0)

            dve.wait_ge(s_small, 80)
            dve.tensor_scalar(qscale[:, :], seq_row[:, :], 0.0, float(DH) ** -0.5, ALU.is_gt,
                              ALU.mult).then_inc(s_dve_const, 1)
            dve.tensor_copy(seq_colf[:, :], seq_col[:, :]).then_inc(s_bias, 1)
            dve.wait_ge(s_pool_const, 8)
            dve.wait_ge(s_bias, 1)
            dve.tensor_scalar(mask_rows[:, :], key_id[:, :], seq_colf[:, 0:1], MASK, ALU.is_ge,
                              ALU.mult).then_inc(s_bias, 1)
            dve.wait_ge(s_bias, 2)
            dve.tensor_tensor(bias_rows[:, :], mask_rows[:, :], b_rows[:, :], ALU.add).then_inc(s_bias, 1)
            dve.wait_ge(s_bias, 3)
            dve.tensor_copy(bias_part[:, 0, :], bias_rows[:, :]).then_inc(s_bias, 1)
            dve.wait_ge(s_bias, 4)
            dve.tensor_tensor(bias_rest[:, :], bias_rows[:, :], bias_part[:, 0, :], ALU.subtract).then_inc(s_bias, 1)
            dve.wait_ge(s_bias, 5)
            dve.tensor_copy(bias_part[:, 1, :], bias_rest[:, :]).then_inc(s_dve_const, 1)
            dve.wait_ge(s_dve_const, 2)
            dve.tensor_tensor(bias_part[:, 2, :], bias_rest[:, :], bias_part[:, 1, :], ALU.subtract).then_inc(s_bias, 1)

            def stats1(p):
                o = NSTAT * p
                if p % 2 == 0:
                    dve.wait_ge(s_x[p // 2], 16)
                for i in range(2):
                    dve.bn_stats(stats[:, i, :], X[:, 2 * p + i, :]).then_inc(s_stat, 1)
                for i in range(2):
                    dve.wait_ge(s_stat, o + i + 1)
                    dve.bn_aggr(mv[:, i, :], stats[:, i, :]).then_inc(s_stat, 1)
                dve.wait_ge(s_stat, o + 4)
                if p >= 2:
                    dve.wait_ge(s_pow, p - 1)
                dve.tensor_scalar(veps[:, p % 2, :], mv[:, :, 1], EPS, None, ALU.add).then_inc(s_stat, 1)

            def scales1(p):
                o = NSTAT * p
                dve.wait_ge(s_pow, p + 1)
                if p >= 2:
                    dve.wait_ge(s_xhat, 2 * (p - 1))
                if p == 0:
                    dve.wait_ge(s_dve_const, 1)
                dve.tensor_tensor(qmul[:, p % 2, :], rstd[:, p % 2, :], qscale[:, 2 * p:2 * p + 2],
                                  ALU.mult).then_inc(s_stat, 1)
                dve.wait_ge(s_stat, o + 6)
                dve.scalar_tensor_tensor(out=qadd[:, p % 2, :], in0=mv[:, :, 0], scalar=-1.0, in1=qmul[:, p % 2, :],
                                         op0=ALU.mult, op1=ALU.mult).then_inc(s_stat, 1)

            def row_max(n, c):
                i, p = CH * n + c, n // 2
                dve.wait_ge(s_sc1, i + 1)
                dve.tensor_reduce(negmax[:, p % 2, n % 2, c * G:(c + 1) * G], bank_cols(sc1[i % 2]), AX.X, ALU.max,
                                  negate=True).then_inc(s_max, 1)

            def split_max(p):
                o = NMS * p
                dve.wait_ge(s_max, 2 * CH * (p + 1))
                if p >= 2:
                    dve.wait_ge(s_mT, p - 1)
                src = negmax[:, p % 2, :, :]
                dst = max_part[:, p % 2, :, :, :]
                dve.tensor_copy(dst[:, :, 0, :], src).then_inc(s_msplit, 1)
                dve.wait_ge(s_msplit, o + 1)
                dve.tensor_tensor(max_rest[:, :, :], src, dst[:, :, 0, :], ALU.subtract).then_inc(s_msplit, 1)
                dve.wait_ge(s_msplit, o + 2)
                dve.tensor_copy(dst[:, :, 1, :], max_rest[:, :, :]).then_inc(s_msplit, 1)
                dve.wait_ge(s_msplit, o + 3)
                dve.tensor_tensor(dst[:, :, 2, :], max_rest[:, :, :], dst[:, :, 1, :],
                                  ALU.subtract).then_inc(s_msplit, 1)

            def add_attention(n):
                o = NNORM * n
                C3 = CH - 1
                if n == 0:
                    dve.wait_ge(s_tanh, 1)
                dve.wait_ge(s_oT, n + 1)
                a = o_t[:, 0:128].rearrange("p (g w) -> p g w", g=G)
                z = o_t[:, 128:256].rearrange("p (g w) -> p g w", g=G)
                sums = a[:, :, 0:9 * C3].rearrange("p g (c w) -> p c g w", c=C3)
                rs = rsum[:, n % 2, :, :]
                on = o_norm[:, n % 2, :, :, :]
                dve.reciprocal(rs[:, 0:C3, :], sums[:, :, :, DH]).then_inc(s_norm, 1)
                dve.reciprocal(rs[:, C3, :], z[:, :, DH]).then_inc(s_norm, 1)
                dve.wait_ge(s_norm, o + 2)
                dve.tensor_tensor(on[:, 0:C3, :, :], sums[:, :, :, 0:DH],
                                  rs[:, 0:C3, :, None].to_broadcast([128, C3, G, DH]), ALU.mult).then_inc(s_norm, 1)
                dve.tensor_tensor(on[:, C3, :, :], z[:, :, 0:DH],
                                  rs[:, C3, :, None].to_broadcast([128, G, DH]), ALU.mult).then_inc(s_norm, 1)
                dve.wait_ge(s_norm, o + 4)
                dve.scalar_tensor_tensor(out=X[:, n, :], in0=on.rearrange("p c g d -> p (c g d)"),
                                         scalar=tanh_g[:, 0:1], in1=X[:, n, :], op0=ALU.mult,
                                         op1=ALU.add).then_inc(s_norm, 1)

            for q in range(-4, PAIRS + 3):
                if 0 <= q + 4 < PAIRS:
                    stats1(q + 4)
                if q in (-3, -2):
                    zero_half(q + 4)
                for i in range(2):
                    m, n = 2 * q + i, 2 * (q - 2) + i
                    for c in range(CH):
                        if 0 <= m < B:
                            row_max(m, c)
                        if c == 2 and 0 <= n - 1 < B:
                            add_attention(n - 1)
                    if i == 0 and 0 <= q + 4 < PAIRS:
                        scales1(q + 4)
                    if q == PAIRS - 3 and i == 1:
                        dve.wait_ge(s_w, 16 * 11)
                        dve.tensor_scalar(nbi_col[:, :], bi_col[:, :], -1.0, None, ALU.mult).then_inc(s_shift, 1)
                        dve.tensor_copy(bi_wide[:, :, :],
                                        bi_col[:, :, None].to_broadcast([128, FC, 128])).then_inc(s_shift, 1)
                if 0 <= q < PAIRS:
                    split_max(q)
            dve.wait_ge(s_wT, 5)
            dve.scalar_tensor_tensor(out=shift[:, :], in0=bo_rows[:, :], scalar=2.0, in1=qk_t[:, 0:D],
                                     op0=ALU.mult, op1=ALU.add).then_inc(s_shift, 1)

            def stats2_of(g):
                o = NST2 * g
                if g >= 1:
                    dve.wait_ge(s_xh2, GT * g)
                for t in range(GT):
                    dve.bn_stats(stats2[:, t, :], X[:, GT * g + t, :]).then_inc(s_stat2, 1)
                for t in range(GT):
                    dve.wait_ge(s_stat2, o + t + 1)
                    dve.bn_aggr(mv2[:, t, :], stats2[:, t, :]).then_inc(s_stat2, 1)
                dve.wait_ge(s_stat2, o + 8)
                dve.tensor_scalar(veps2[:, :], mv2[:, :, 1], EPS, None, ALU.add).then_inc(s_stat2, 1)

            def shifts2(g):
                dve.wait_ge(s_pow2, g + 1)
                dve.scalar_tensor_tensor(out=nmean2[:, :], in0=mv2[:, :, 0], scalar=-1.0, in1=rstd2[:, :],
                                         op0=ALU.mult, op1=ALU.mult).then_inc(s_stat2, 1)

            def wide(t):
                return t[:, :, None].to_broadcast([128, GT, E])

            steps = [0]

            def gate_step(ins):
                steps[0] += 1
                ins.then_inc(s_gate, 1)

            def last_step():
                dve.wait_ge(s_gate, steps[0])

            def gates_shift(g):
                dve.wait_ge(s_ug, g + 1)
                for i in range(2):
                    src = bank[3 + i][:, 0:2 * UW].rearrange("p (t w) -> p t w", t=2)[:, :, E * R:UW]
                    gate_step(dve.tensor_tensor(lg[:, 2 * i:2 * i + 2, :], src,
                                                gb_rows[:, None, :].to_broadcast([128, 2, E]), ALU.add))
                last_step()
                gate_step(dve.tensor_reduce(lmax[:, :], lg[:, :, :], AX.X, ALU.max))
                last_step()
                if g >= 1:
                    dve.wait_ge(s_gexp, g)
                gate_step(dve.tensor_tensor(lsh[:, :, :], lg[:, :, :], wide(lmax), ALU.subtract))

            def gates_pick(g):
                dve.wait_ge(s_gexp, g + 1)
                gate_step(dve.tensor_reduce(lsum[:, :], lexp[:, :, :], AX.X, ALU.add))
                last_step()
                gate_step(dve.reciprocal(lmax[:, :], lsum[:, :]))
                last_step()
                gate_step(dve.tensor_tensor(score[:, :, :], lexp[:, :, :], wide(lmax), ALU.mult))
                for i in range(2):
                    last_step()
                    gate_step(dve.tensor_reduce(top[:, i, :], score[:, :, :], AX.X, ALU.max))
                    last_step()
                    gate_step(dve.tensor_tensor(tie[:, :, :], score[:, :, :], wide(top[:, i, :]), ALU.is_equal))
                    last_step()
                    gate_step(dve.tensor_tensor(lg[:, :, :], tie[:, :, :],
                                                first[:, None, :].to_broadcast([128, GT, E]), ALU.mult))
                    last_step()
                    gate_step(dve.tensor_reduce(key[:, :], lg[:, :, :], AX.X, ALU.max))
                    last_step()
                    gate_step(dve.tensor_tensor(hot[:, i, :, :], lg[:, :, :], wide(key), ALU.is_equal))
                    if i == 0:
                        last_step()
                        gate_step(dve.scalar_tensor_tensor(
                            out=score[:, :, :].rearrange("p t e -> p (t e)"),
                            in0=hot[:, 0, :, :].rearrange("p t e -> p (t e)"), scalar=-2.0,
                            in1=score[:, :, :].rearrange("p t e -> p (t e)"), op0=ALU.mult, op1=ALU.add))
                gate_step(dve.tensor_tensor(lsum[:, :], top[:, 0, :], top[:, 1, :], ALU.add))
                last_step()
                gate_step(dve.tensor_tensor(hot_diff[:, :, :], hot[:, 1, :, :], hot[:, 0, :, :], ALU.subtract))
                gate_step(dve.tensor_scalar(gate[:, g % 2, :], lsum[:, :], tanh_g[:, 1:2], None, ALU.mult))

            def mask_u(g):
                last_step()
                if g >= 1:
                    dve.wait_ge(s_uT, 2 * g)
                for k, m in enumerate((hot[:, 0, :, :], hot_diff[:, :, :])):
                    for i in range(2):
                        for_tiles = bank[3 + i][:, 0:2 * UW].rearrange("p (t w) -> p t w", t=2)[:, :, 0:E * R]
                        dve.tensor_tensor(u[:, k, 2 * i:2 * i + 2, :, :],
                                          for_tiles.rearrange("p t (e r) -> p t e r", e=E),
                                          m[:, 2 * i:2 * i + 2, :, None].to_broadcast([128, 2, E, R]),
                                          ALU.mult).then_inc(s_u, 1)

            def sum_experts(g, c):
                i = FC * g + c
                dve.wait_ge(s_d, i + 1)
                dve.scalar_tensor_tensor(out=hsum[:, c, :], in0=chunk_bank(i)[:, :], scalar=nbi_col[:, c:c + 1],
                                         in1=h1[:, i % 2, :], op0=ALU.max, op1=ALU.add).then_inc(s_hs, 1)

            def finish(g):
                o = NFIN * g
                if g >= 2:
                    dve.wait_ge(s_out[g % 2], 16 * (g // 2))
                for t in range(GT):
                    dve.scalar_tensor_tensor(out=base[:, t, :], in0=shift[:, :], scalar=gate[:, g % 2, t:t + 1],
                                             in1=X[:, GT * g + t, :], op0=ALU.mult, op1=ALU.add).then_inc(s_fin, 1)
                dve.wait_ge(s_o, g + 1)
                for t in range(GT):
                    dve.wait_ge(s_fin, o + t + 1)
                    dve.scalar_tensor_tensor(out=res[:, g % 2, t, :], in0=bank_out[:, t * 128:(t + 1) * 128],
                                             scalar=gate[:, g % 2, t:t + 1], in1=base[:, t, :], op0=ALU.mult,
                                             op1=ALU.add).then_inc(s_fin, 1)

            dve.wait_ge(s_norm, NNORM * B)
            for g in range(-2, GROUPS):
                if g + 2 < GROUPS:
                    stats2_of(g + 2)
                if 0 <= g + 1 < GROUPS:
                    gates_shift(g + 1)
                if g >= 0:
                    sum_experts(g, 0)
                if 0 <= g + 1 < GROUPS:
                    gates_pick(g + 1)
                if g + 2 < GROUPS:
                    shifts2(g + 2)
                if g >= 0:
                    sum_experts(g, 1)
                if 0 <= g + 1 < GROUPS:
                    mask_u(g + 1)
                if g >= 0:
                    sum_experts(g, 2)
                    sum_experts(g, 3)
                    finish(g)


_INS = ["x", "ctx_2048", "itok_Bx1_68_817", "g_xattn", "g_ffn", "L0_xattn_b", "L0_ffn_wi", "L0_ffn_bi", "L0_ffn_wo",
        "L0_ffn_bo", "L0_ffn_lora_A", "L0_ffn_lora_B", "L0_ffn_gate_w", "L0_ffn_gate_b"]


def kernel(**inputs):
    import numpy as _np
    import concourse.bacc as _bacc
    from concourse import mybir as _mybir
    from concourse.bass_utils import run_bass_kernel_spmd as _run

    nc = _bacc.Bacc("TRN2", target_bir_lowering=False, num_devices=1)
    arrays, args = {}, []
    for name in _INS:
        a = _np.ascontiguousarray(inputs[name])
        arrays[f"in_{name}_dram"] = a
        args.append(nc.dram_tensor(f"in_{name}_dram", a.shape, _mybir.dt.from_np(a.dtype), kind="ExternalInput").ap())
    shape = inputs["x"].shape
    args.append(nc.dram_tensor("out_0_dram", shape, _mybir.dt.float32, kind="ExternalOutput").ap())
    flamingo(nc, *args)
    r = _run(nc, [arrays], core_ids=[0])
    return r.results[0]["out_0_dram"]
```

```python
from contextlib import ExitStack

import concourse.bass as bass
from concourse import mybir

ALU = mybir.AluOpType
ACT = mybir.ActivationFunctionType
AX = mybir.AxisListType
F32 = mybir.dt.float32
F32R = mybir.dt.float32r
BF16 = mybir.dt.bfloat16
I32 = mybir.dt.int32

MASK = -1.0e12
EPS = 1.0e-5

QPART = [0, 0, 1, 1, 0, 2]
KPART = [0, 1, 0, 1, 2, 0]
TERM_STEP = 15
BIAS_ROW = 120
MAX_ROW = 125
PARTS = 3


def flamingo(nc, x, ctx, seq_len, g_xattn, g_ffn, b, wi, bi, wo, bo, lora_a, lora_b, gate_w, gate_b, out):
    B, S, D = x.shape
    H = 16
    DH = D // H
    F = wi.shape[0]
    E, R, _ = lora_a.shape
    FC = F // 128
    PAIRS = B // 2
    QUADS = B // 4
    SLOTS = 3
    CH = 4
    G = 4
    GT = 4
    GROUPS = B // GT
    UW = E * R + E
    STACK_DMAS = 11

    es = ExitStack()
    with es:
        def sb(name, shape, dt):
            return es.enter_context(nc.sbuf_tensor(name, shape, dt))

        def psum(name, shape, dt):
            return es.enter_context(nc.psum_tensor(name, shape, dt))

        def sem(name):
            return es.enter_context(nc.semaphore(name))

        X = sb("X", [128, B, D], F32)
        V = sb("V", [128, B, D], F32)
        ident = sb("ident", [128, 128], F32)
        identb = sb("identb", [128, 128], BF16)
        onesb = sb("onesb", [128, 512], BF16)
        zeros = sb("zeros", [128, 1], F32)
        half_neg = sb("half_neg", [128, B], F32)
        seq_row = sb("seq_row", [128, B], I32)
        qscale = sb("qscale", [128, B], F32)
        gates = sb("gates", [128, 2], F32)
        tanh_g = sb("tanh_g", [128, 2], F32)
        seq_col = sb("seq_col", [B, 1], I32)
        seq_colf = sb("seq_colf", [B, 1], F32)
        key_id = sb("key_id", [B, S], F32)
        b_rows = sb("b_rows", [B, S], F32)
        mask_rows = sb("mask_rows", [B, S], F32)
        bias_rows = sb("bias_rows", [B, S], F32)
        bias_rest = sb("bias_rest", [B, S], F32)
        bias_part = sb("bias_part", [B, PARTS, S], BF16)
        bias_line = sb("bias_line", [PARTS, B * S], BF16)
        kin = sb("kin", [128, 2, 4, D], F32)
        stats = sb("stats", [128, B, 6], F32)
        mv = sb("mv", [128, B, 2], F32)
        veps = sb("veps", [128, B], F32)
        rstd = sb("rstd", [128, B], F32)
        qmul = sb("qmul", [128, B], F32)
        qadd = sb("qadd", [128, B], F32)
        xhat = sb("xhat", [128, 2, 2, D], F32)
        kperm = sb("kperm", [128, 2, 2, D], F32)
        full = sb("full", [128, 512], F32)
        rest = sb("rest", [128, 512], F32)
        part = [sb(f"part{i}", [128, 2, 2, 512], BF16) for i in range(PARTS)]
        negmax = sb("negmax", [128, 2, 2, H], F32)
        max_rest = sb("max_rest", [128, 2, H], F32)
        max_part = sb("max_part", [128, 2, 2, PARTS, H], BF16)
        max_rows = sb("max_rows", [PARTS * H, 2, 256], BF16)
        probs = sb("probs", [128, 4, 512], F32)
        vpad = sb("vpad", [128, 2, CH * 137], F32)
        o_rows = sb("o_rows", [128, 2, 256], F32)
        rsum = sb("rsum", [128, 2, CH, G], F32)
        o_norm = sb("o_norm", [128, 2, CH, G, DH], F32)
        V_SPENT = 3 * FC + 1
        wi_in = V[:, 0:FC, :]
        wo_in = V[:, FC:2 * FC, :].rearrange("p c d -> p (c d)")
        b_in = V[:, 2 * FC:3 * FC, :].rearrange("p c (e r) -> p c e r", e=E)
        a_in = V[:, 3 * FC, :]
        gw_in = sb("gw_in", [E, D], F32)
        wiT = sb("wiT", [128, FC, 128], F32)
        woT = sb("woT", [128, FC, 128], F32)
        bT = sb("bT", [128, FC, 128], F32)
        wi_part = sb("wi_part", [128, 2, FC, 128], F32R)
        b_part = sb("b_part", [128, 2, FC, 128], F32R)
        agT = sb("agT", [128, UW], F32)
        bi_col = sb("bi_col", [128, FC], F32)
        nbi_col = sb("nbi_col", [128, FC], F32)
        bi_wide = sb("bi_wide", [128, FC, 128], F32)
        bo_rows = sb("bo_rows", [128, D], F32)
        shift = sb("shift", [128, D], F32)
        gb_rows = sb("gb_rows", [128, E], F32)
        first = sb("first", [128, E], F32)
        stats2 = sb("stats2", [128, GT, 6], F32)
        mv2 = sb("mv2", [128, GT, 2], F32)
        veps2 = sb("veps2", [128, GT], F32)
        rstd2 = sb("rstd2", [128, GT], F32)
        nmean2 = sb("nmean2", [128, GT], F32)
        lg = sb("lg", [128, GT, E], F32)
        lmax = sb("lmax", [128, GT], F32)
        lsh = sb("lsh", [128, GT, E], F32)
        lexp = sb("lexp", [128, GT, E], F32)
        lsum = sb("lsum", [128, GT], F32)
        score = sb("score", [128, GT, E], F32)
        top = sb("top", [128, 2, GT], F32)
        tie = sb("tie", [128, GT, E], F32)
        key = sb("key", [128, GT], F32)
        hot = sb("hot", [128, 2, GT, E], F32)
        hot_diff = sb("hot_diff", [128, GT, E], F32)
        gate = sb("gate", [128, 2, GT], F32)

        lent = ExitStack()
        stack = lent.enter_context(nc.sbuf_tensor("stack", [128, SLOTS, H, 1024], BF16))
        lent.close()
        xhat2 = sb("xhat2", [128, GT, D], F32)
        xT = sb("xT", [128, 2, 512], F32)
        x_part = sb("x_part", [128, 2, 2, 512], F32R)
        u = sb("u", [128, 2, GT, E, R], F32)
        u_part = sb("u_part", [128, 2, 2, 512], F32R)
        base = sb("base", [128, GT, D], F32)
        h1 = sb("h1", [128, FC, 512], F32)
        hsum = sb("hsum", [128, FC, 512], F32)
        res = sb("res", [128, 2, GT, D], F32)

        bank = [psum(f"bank{i}", [128, 512], F32) for i in range(7)]
        bank_max = psum("bank_max", [128, 1024], BF16)
        sc1 = bank[0:2]
        sc2 = bank[2:4]
        o_acc, qk_t, o_t = bank[4:7]
        bank_out = bank_max[:, :].bitcast(F32)

        s_x = [sem(f"s_x{i}") for i in range(QUADS)]
        s_v = [sem(f"s_v{i}") for i in range(QUADS)]
        s_k = [sem(f"s_k{i}") for i in range(2)]
        s_seq = sem("s_seq")
        s_b = sem("s_b")
        s_gates = sem("s_gates")
        s_w = sem("s_w")
        s_pool_const = sem("s_pool_const")
        s_dve_const = sem("s_dve_const")
        s_bias = sem("s_bias")
        s_line = sem("s_line")
        s_zero = [sem(f"s_zero{i}") for i in range(SLOTS)]
        s_fixed = [sem(f"s_fixed{i}") for i in range(SLOTS)]
        s_tanh = sem("s_tanh")
        s_wT = sem("s_wT")
        s_wTc = sem("s_wTc")
        s_shift = sem("s_shift")
        s_stat = sem("s_stat")
        s_var = sem("s_var")
        s_scale = sem("s_scale")
        s_pow = sem("s_pow")
        s_kperm = sem("s_kperm")
        s_xhat = sem("s_xhat")
        s_qkT = sem("s_qkT")
        s_t1 = sem("s_t1")
        s_full = sem("s_full")
        s_rest = sem("s_rest")
        s_t2 = sem("s_t2")
        s_t3 = sem("s_t3")
        s_stack = [sem(f"s_stack{i}") for i in range(SLOTS)]
        s_maxrow = [sem(f"s_maxrow{i}") for i in range(4)]
        s_sc1 = sem("s_sc1")
        s_max = sem("s_max")
        s_msplit = sem("s_msplit")
        s_mT = sem("s_mT")
        s_mTc = sem("s_mTc")
        s_sc2 = sem("s_sc2")
        s_exp = sem("s_exp")
        s_vpad = sem("s_vpad")
        s_pv = sem("s_pv")
        s_oc = sem("s_oc")
        s_oT = sem("s_oT")
        s_norm = sem("s_norm")
        s_stat2 = sem("s_stat2")
        s_pow2 = sem("s_pow2")
        s_xh2 = sem("s_xh2")
        s_xT = sem("s_xT")
        s_xTc = sem("s_xTc")
        s_ug = sem("s_ug")
        s_gate = sem("s_gate")
        s_gexp = sem("s_gexp")
        s_u = sem("s_u")
        s_uT = sem("s_uT")
        s_uTc = sem("s_uTc")
        s_w_lo = sem("s_w_lo")
        s_x_hi = sem("s_x_hi")
        s_x_lo = sem("s_x_lo")
        s_u_lo = sem("s_u_lo")
        s_a = sem("s_a")
        s_h1 = sem("s_h1")
        s_d = sem("s_d")
        s_hs = sem("s_hs")
        s_o = sem("s_o")
        s_fin = sem("s_fin")
        s_gated = sem("s_gated")
        s_base = sem("s_base")
        s_out = [sem("s_out0"), sem("s_out1")]

        LEAD = 4
        WEIGHTS_AT = PAIRS - LEAD + 1
        BATCHES = [(0, 4), (4, 8), (8, 16), (16, 24), (24, B)]
        NNORM = 5
        NMS = 4
        NST2 = 10
        NGATE = 21
        NFIN = GT
        POOL_CONSTS = 10

        words = stack[:, :, :, :].bitcast(F32)

        def pair_cols(t, p):
            return t[:, (p // 2) % 2, :, 256 * (p % 2):256 * (p % 2) + 256]

        def halves(t):
            return t[:, :].rearrange("p (s c) -> p s c", s=2)

        def v_window(n, c, g):
            at = (c * G + g) * 32
            return vpad[:, n % 2, at:at + 32]

        def v_column(c):
            return (DH + 1) * c if c < CH - 1 else 0

        def chunk_bank(i):
            return bank[2 + i % 3]

        def ug_bank(t):
            return bank[t // 2]

        def bank_cols(t):
            return t[:, :].rearrange("p (j k) -> p j k", j=G)

        block = es.enter_context(nc.Block())

        @block.sync
        def _(sp):
            ctx_t = ctx.rearrange("b s d -> s b d")
            x_t = x.rearrange("b s d -> s b d")

            def load_k(Q):
                if Q >= 2:
                    sp.wait_ge(s_kperm, 2 * (Q - 1))
                sp.dma_start(kin[:, Q % 2, :, :], ctx_t[:, 4 * Q:4 * Q + 4, 0:D]).then_inc(s_k[Q % 2], 16)

            def load_x(Q):
                sp.dma_start(X[:, 4 * Q:4 * Q + 4, :], x_t[:, 4 * Q:4 * Q + 4, :]).then_inc(s_x[Q], 16)

            def load_v(Q):
                sp.dma_start(V[:, 4 * Q:4 * Q + 4, :], ctx_t[:, 4 * Q:4 * Q + 4, D:2 * D]).then_inc(s_v[Q], 16)

            def rows_of_ones(s):
                sp.wait_ge(s_zero[s], 4)
                sp.dma_start(stack[BIAS_ROW:BIAS_ROW + PARTS, s, :, 0:512],
                             onesb[0:PARTS, None, :].to_broadcast([PARTS, H, 512])).then_inc(s_fixed[s], 16)
                sp.dma_start(stack[MAX_ROW:MAX_ROW + PARTS, s, :, 512:1024],
                             onesb[0:PARTS, None, :].to_broadcast([PARTS, H, 512])).then_inc(s_fixed[s], 16)

            def rows(s, r, lo, hi):
                return stack[r:r + TERM_STEP * (DH - 1) + 1:TERM_STEP, s, :, lo:hi]

            def bias_to_stack(Q):
                if Q >= SLOTS:
                    sp.wait_ge(s_sc2, 4 * CH * (Q - SLOTS + 1))
                sp.dma_start(stack[BIAS_ROW:BIAS_ROW + PARTS, Q % SLOTS, :, 512:1024],
                             bias_line[:, None, 512 * Q:512 * Q + 512].to_broadcast([PARTS, H, 512])
                             ).then_inc(s_stack[Q % SLOTS], 16)

            def part_to_stack(Q, i, products=range(len(QPART))):
                s, t = Q % SLOTS, Q % 2
                sp.wait_ge((s_t1, s_t2, s_t3)[i], 2 * (Q + 1))
                for r in products:
                    if QPART[r] == i and KPART[r] == i:
                        sp.dma_start(rows(s, r, 0, 1024),
                                     part[i][:, t, :, :].rearrange("p s c -> p (s c)")).then_inc(s_stack[s], 16)
                    elif QPART[r] == i:
                        sp.dma_start(rows(s, r, 0, 512), part[i][:, t, 0, :]).then_inc(s_stack[s], 16)
                    elif KPART[r] == i:
                        sp.dma_start(rows(s, r, 512, 1024), part[i][:, t, 1, :]).then_inc(s_stack[s], 16)

            def max_to_stack(p):
                sp.wait_ge(s_mTc, p + 1)
                c0 = 256 * (p % 2)
                sp.dma_start(stack[MAX_ROW:MAX_ROW + PARTS, (p // 2) % SLOTS, :, c0:c0 + 256],
                             max_rows[:, p % 2, :]).then_inc(s_maxrow[p % 4], 16)

            def load_weights():
                sp.wait_ge(s_vpad, 2 * CH + 2 * V_SPENT)
                sp.dma_start(wi_in[:, :, :], wi.rearrange("(c p) d -> p c d", p=128)).then_inc(s_w, 16)
                sp.dma_start(wo_in[:, :], wo).then_inc(s_w, 16)
                for c in range(FC):
                    sp.dma_start(b_in[:, c, :, :],
                                 lora_b[:, c * 128:(c + 1) * 128, :].rearrange("e p r -> p e r")).then_inc(s_w, 16)
                sp.dma_start(a_in[:, :], lora_a.rearrange("e r d -> (e r) d")).then_inc(s_w, 16)
                sp.dma_start(gw_in[:, :], gate_w).then_inc(s_w, 16)
                with nc.allow_non_contiguous_dma(reason="512 biases to columns, once"):
                    sp.dma_start(bi_col[:, :], bi.rearrange("(c p) -> p c", p=128)).then_inc(s_w, 16)
                sp.dma_start(bo_rows[:, :], bo.rearrange("(o k) -> o k", o=1).to_broadcast([128, D])).then_inc(s_w, 16)
                sp.dma_start(gb_rows[:, :], gate_b.rearrange("(o k) -> o k", o=1).to_broadcast([128, E])).then_inc(s_w, 16)

            load_x(0)
            load_k(0)
            load_x(1)
            load_k(1)
            sp.dma_start(b_rows[:, :], b.rearrange("(o k) -> o k", o=1).to_broadcast([B, S])).then_inc(s_b, 16)
            for Q in range(2, QUADS):
                load_x(Q)
            sp.wait_ge(s_bias, 6)
            for i in range(PARTS):
                sp.dma_start(bias_line[i:i + 1, :].rearrange("p (b k) -> p b k", b=B),
                             bias_part[:, i, :]).then_inc(s_line, 16)
            sp.wait_ge(s_pool_const, 4)
            for Q in range(LEAD // 2):
                rows_of_ones(Q)
                if Q == 0:
                    sp.wait_ge(s_line, 16 * PARTS)
                bias_to_stack(Q)
                for i in range(PARTS):
                    part_to_stack(Q, i)
                load_v(Q)
                load_k(Q + 2)

            for q in range(PAIRS + 1):
                Q = q // 2 + 1
                if q % 2 == 1 and LEAD // 2 <= Q < QUADS:
                    part_to_stack(Q, 1)
                    part_to_stack(Q, 2)
                if q % 2 == 0 and LEAD // 2 <= Q < QUADS:
                    bias_to_stack(Q)
                    part_to_stack(Q, 0, range(3))
                if q >= 1:
                    max_to_stack(q - 1)
                if q == 1:
                    rows_of_ones(SLOTS - 1)
                if q % 2 == 0 and LEAD // 2 <= Q < QUADS:
                    part_to_stack(Q, 0, range(3, len(QPART)))
                    if Q + 2 < QUADS:
                        load_k(Q + 2)
                    load_v(Q)
                if q == 9:
                    load_weights()

            for g in range(GROUPS):
                sp.wait_ge(s_fin, NFIN * (g + 1))
                sp.dma_start(out.rearrange("b s d -> s b d")[:, GT * g:GT * g + GT, :],
                             res[:, g % 2, :, :]).then_inc(s_out[g % 2], 16)
            sp.wait_ge(s_out[0], 16 * (GROUPS // 2))
            sp.wait_ge(s_out[1], 16 * (GROUPS // 2))

        @block.gpsimd
        def _(pool):
            pool.memset(zeros[:, :], 0.0).then_inc(s_pool_const, 1)
            pool.memset(ident[:, :], 0.0).then_inc(s_pool_const, 1)
            pool.memset(identb[:, :], 0.0).then_inc(s_pool_const, 1)
            pool.memset(onesb[:, :], 1.0).then_inc(s_pool_const, 1)
            pool.wait_ge(s_pool_const, 3)
            for m in (ident, identb):
                pool.affine_select(out=m[:, :], in_=m[:, :], compare_op=ALU.not_equal, fill=1.0, base=0,
                                   pattern=[[-1, 128]], channel_multiplier=1).then_inc(s_pool_const, 1)
            pool.memset(half_neg[:, :], -0.5).then_inc(s_pool_const, 1)
            pool.iota(key_id[:, :], pattern=[[1, S]], base=0, channel_multiplier=0,
                      allow_small_or_imprecise_dtypes=True).then_inc(s_pool_const, 1)
            pool.iota(first[:, :], pattern=[[-1, E]], base=E, channel_multiplier=0,
                      allow_small_or_imprecise_dtypes=True).then_inc(s_pool_const, 1)

            def ones_beside_v():
                pool.memset(vpad[:, :, :], 0.0).then_inc(s_pool_const, 1)
                pool.wait_ge(s_pool_const, POOL_CONSTS)
                for s in range(2):
                    for c in range(CH):
                        for g in range(G):
                            at = (c * G + g) * 32 + v_column(c) + DH
                            last = pool.memset(vpad[:, s, at:at + 1], 1.0)
                        last.then_inc(s_vpad, 1)

            def perm(t):
                return t.rearrange("p b (h d) -> p b d h", h=H)

            def rsqrt(k):
                lo, hi = BATCHES[k]
                pool.wait_ge(s_var, k + 1)
                if k == 0:
                    pool.wait_ge(s_pool_const, 7)
                pool.tensor_tensor(rstd[:, lo:hi], veps[:, lo:hi], half_neg[:, lo:hi], ALU.pow).then_inc(s_pow, 1)

            def permute_k(p):
                pool.wait_ge(s_k[(p // 2) % 2], 16 * (p // 4 + 1))
                if p >= 2:
                    pool.wait_ge(s_qkT, p - 1)
                pool.tensor_copy(kperm[:, p % 2, :, :].rearrange("p b (d h) -> p b d h", h=H),
                                 perm(kin[:, (p // 2) % 2, 2 * (p % 2):2 * (p % 2) + 2, :])).then_inc(s_kperm, 1)

            def normalise(p):
                batch = [2 * p < hi for lo, hi in BATCHES].index(True)
                pool.wait_ge(s_scale, 2 * (batch + 1))
                if p >= 2:
                    pool.wait_ge(s_qkT, p - 1)
                for i in range(2):
                    pool.tensor_scalar(xhat[:, p % 2, i, :].rearrange("p (d h) -> p d h", h=H),
                                       X[:, 2 * p + i, :].rearrange("p (h d) -> p d h", h=H),
                                       qmul[:, 2 * p + i:2 * p + i + 1], qadd[:, 2 * p + i:2 * p + i + 1],
                                       ALU.mult, ALU.add).then_inc(s_xhat, 1)

            def place_v(n):
                if n % 4 == 0:
                    pool.wait_ge(s_v[n // 4], 16)
                if n >= 2:
                    pool.wait_ge(s_pv, CH * (n - 1))
                else:
                    pool.wait_ge(s_vpad, 2 * CH)
                v = V[:, n, :].rearrange("p (c g d) -> p c g d", c=CH, g=G)
                dst = vpad[:, n % 2, :].rearrange("p (c w) -> p c w", c=CH)[:, 0:CH - 1, 0:128]
                pool.tensor_copy(dst.rearrange("p c (g w) -> p c g w", g=G)[:, :, :, 0:DH],
                                 v[:, 0:CH - 1, :, :]).then_inc(s_vpad, 1)
                dst = vpad[:, n % 2, 128 * (CH - 1):128 * CH].rearrange("p (g w) -> p g w", g=G)
                pool.tensor_copy(dst[:, :, 0:DH], v[:, CH - 1, :, :]).then_inc(s_vpad, 1)

            def first_rest(p):
                pool.wait_ge(s_full, p - LEAD + 1)
                pool.wait_ge(s_t2, p)
                pool.wait_ge(s_t3, p)
                pool.tensor_tensor(halves(rest), halves(full), pair_cols(part[0], p), ALU.subtract).then_inc(s_rest, 1)

            def third_part(p):
                pool.wait_ge(s_t2, p + 1)
                pool.tensor_tensor(pair_cols(part[2], p), halves(rest), pair_cols(part[1], p),
                                   ALU.subtract).then_inc(s_t3, 1)

            def weight_low(whole, parts, ready):
                pool.wait_ge(s_wTc, ready)
                pool.tensor_tensor(parts[:, 1, :, :], whole[:, :, :], parts[:, 0, :, :], ALU.subtract).then_inc(s_w_lo, 1)

            def rsqrt2(g):
                pool.wait_ge(s_stat2, NST2 * g + 9)
                pool.tensor_tensor(rstd2[:, :], veps2[:, :], half_neg[:, 0:GT], ALU.pow).then_inc(s_pow2, 1)

            def x_low(g):
                pool.wait_ge(s_x_hi, g + 1)
                pool.tensor_tensor(x_part[:, g % 2, 1, :], xT[:, g % 2, :], x_part[:, g % 2, 0, :],
                                   ALU.subtract).then_inc(s_x_lo, 1)

            def make_base(g):
                pool.wait_ge(s_gate, NGATE * (g + 1))
                if g == 0:
                    pool.wait_ge(s_shift, 3)
                else:
                    pool.wait_ge(s_fin, NFIN * g)
                pool.tensor_tensor(base[:, :, :], gate[:, g % 2, :, None].to_broadcast([128, GT, D]),
                                   shift[:, None, :].to_broadcast([128, GT, D]), ALU.mult).then_inc(s_gated, 1)
                pool.wait_ge(s_gated, g + 1)
                pool.tensor_tensor(base[:, :, :], base[:, :, :], X[:, GT * g:GT * (g + 1), :],
                                   ALU.add).then_inc(s_base, 1)

            for p in range(LEAD):
                permute_k(p)
                if p < 2:
                    rsqrt(p)
                normalise(p)
            pool.memset(words[:, 1, 0:H // 4, :], 0.0).then_inc(s_zero[1], 1)
            rsqrt(2)
            ones_beside_v()

            for q in range(PAIRS + 3):
                if q + 4 < PAIRS:
                    if q in (4, 8):
                        rsqrt(2 + q // 4)
                    permute_k(q + 4)
                if q == PAIRS:
                    rsqrt2(0)
                if 0 <= 2 * q - 3 < B:
                    place_v(2 * q - 3)
                if q + 4 < PAIRS:
                    normalise(q + 4)
                if LEAD <= q + 3 < PAIRS:
                    first_rest(q + 3)
                if 0 <= 2 * q - 2 < B:
                    place_v(2 * q - 2)
                if q == PAIRS:
                    rsqrt2(1)
                if LEAD <= q + 3 < PAIRS:
                    third_part(q + 3)
                if q == WEIGHTS_AT + 1:
                    weight_low(wiT, wi_part, 2)
                if q == WEIGHTS_AT + 2:
                    weight_low(bT, b_part, 5)
                if q == PAIRS + 1:
                    rsqrt2(2)
                    x_low(0)

            for g in range(GROUPS):
                if g + 3 < GROUPS:
                    rsqrt2(g + 3)
                if g + 1 < GROUPS:
                    x_low(g + 1)
                make_base(g)

        @block.scalar
        def _(act):
            act.dma_start(seq_row[:, :], seq_len.rearrange("b o -> o b").to_broadcast([128, B])).then_inc(s_seq, 16)
            act.dma_start(seq_col[:, :], seq_len).then_inc(s_seq, 16)
            act.dma_start(gates[:, 0:1], g_xattn.rearrange("(o k) -> o k", o=1).to_broadcast([128, 1])).then_inc(s_gates, 16)
            act.dma_start(gates[:, 1:2], g_ffn.rearrange("(o k) -> o k", o=1).to_broadcast([128, 1])).then_inc(s_gates, 16)

            def zero(s, quarter):
                dst = words[:, s, H // 4 * quarter:H // 4 * (quarter + 1), :]
                act.activation(dst, zeros[:, 0:1, None].to_broadcast([128, H // 4, 512]), ACT.Copy).then_inc(s_zero[s], 1)

            def copy_weights(i):
                dst = (wiT, woT, bT)[i][:, :, :].rearrange("p c f -> p (c f)") if i < 3 else agT[:, :]
                act.wait_ge(s_wT, i + 1)
                act.activation(dst, qk_t[:, 0:dst.shape[1]], ACT.Copy).then_inc(s_wTc, 1)
                if i in (0, 2):
                    hi = (wi_part, None, b_part)[i][:, 0, :, :].rearrange("p c f -> p (c f)")
                    act.activation(hi, qk_t[:, :], ACT.Copy).then_inc(s_wTc, 1)

            def first_part(p):
                act.wait_ge(s_qkT, p + 1)
                if p >= 4:
                    old = p // 2 - 2
                    act.wait_ge(s_stack[old % SLOTS], 16 * STACK_DMAS * (old // SLOTS + 1))
                act.activation(pair_cols(part[0], p), halves(qk_t), ACT.Copy).then_inc(s_t1, 1)

            def float_copy(p):
                act.wait_ge(s_rest, p)
                act.activation(full[:, :], qk_t[:, :], ACT.Copy).then_inc(s_full, 1)

            def second_part(p):
                act.wait_ge(s_rest, p + 1)
                act.activation(pair_cols(part[1], p), halves(rest), ACT.Copy).then_inc(s_t2, 1)

            def exps(n, c):
                i = CH * n + c
                act.wait_ge(s_sc2, i + 1)
                if i >= 4:
                    act.wait_ge(s_pv, i - 3)
                act.activation(probs[:, i % 4, :], sc2[i % 2][:, :], ACT.Exp).then_inc(s_exp, 1)

            def copy_o(n):
                act.wait_ge(s_pv, CH * (n + 1))
                if n >= 2:
                    act.wait_ge(s_oT, n - 1)
                act.activation(o_rows[:, n % 2, :], o_acc[:, 0:256], ACT.Copy).then_inc(s_oc, 1)

            def copy_max(p):
                act.wait_ge(s_mT, p + 1)
                if p >= 2:
                    act.wait_ge(s_maxrow[(p - 2) % 4], 16 * ((p - 2) // 4 + 1))
                act.activation(max_rows[:, p % 2, :], bank_max[0:PARTS * H, 0:256], ACT.Copy).then_inc(s_mTc, 1)

            def normalise(g):
                act.wait_ge(s_stat2, NST2 * (g + 1))
                act.wait_ge(s_pow2, g + 1)
                if g >= 1:
                    act.wait_ge(s_xT, g)
                for t in range(GT):
                    act.activation(xhat2[:, t, :], X[:, GT * g + t, :], ACT.Identity, bias=nmean2[:, t:t + 1],
                                   scale=rstd2[:, t:t + 1]).then_inc(s_xh2, 1)

            def copy_xT(g):
                act.wait_ge(s_xT, g + 1)
                if g >= 2:
                    act.wait_ge(s_ug, g - 1)
                    act.wait_ge(s_x_lo, g - 1)
                act.activation(xT[:, g % 2, :], qk_t[:, :], ACT.Copy).then_inc(s_xTc, 1)

            def x_high(g):
                act.wait_ge(s_xTc, g + 1)
                if g >= 2:
                    act.wait_ge(s_d, FC * (g - 1))
                act.activation(x_part[:, g % 2, 0, :], xT[:, g % 2, :], ACT.Copy).then_inc(s_x_hi, 1)

            def gate_exp(g):
                act.wait_ge(s_gate, NGATE * g + 4)
                act.activation(lexp[:, :, :], lsh[:, :, :], ACT.Exp).then_inc(s_gexp, 1)

            def copy_uT(g):
                for i, src in enumerate((qk_t, o_t)):
                    act.wait_ge(s_uT, 2 * g + i + 1)
                    if g >= 1:
                        act.wait_ge(s_d, FC * g)
                    act.activation(u_part[:, i, 0, :], src[:, :], ACT.Copy).then_inc(s_uTc, 1)

            def relu(g, c):
                i = FC * g + c
                act.wait_ge(s_a, i + 1)
                if g >= 1:
                    act.wait_ge(s_hs, i - FC + 1)
                act.activation(h1[:, c, :], chunk_bank(i)[:, :], ACT.Relu,
                               bias=bi_col[:, c:c + 1]).then_inc(s_h1, 1)

            act.wait_ge(s_pool_const, 1)
            zero(0, 2)
            zero(0, 3)
            for p in range(LEAD):
                first_part(p)
                if p == 1:
                    zero(1, p)
                second_part(p)
                if p >= 2:
                    zero(1, p)
            act.wait_ge(s_gates, 32)
            act.activation(tanh_g[:, :], gates[:, :], ACT.Tanh).then_inc(s_tanh, 1)
            for quarter in range(4):
                zero(2, quarter)
            for q in range(PAIRS + 3):
                for i in range(2):
                    n = 2 * (q - 2) + i
                    for c in range(CH):
                        if 0 <= n < B:
                            exps(n, c)
                        if c == 1 and 0 <= n - 1 < B:
                            copy_o(n - 1)
                        if i == 0:
                            if c == 2 and LEAD <= q + 3 < PAIRS:
                                first_part(q + 3)
                            if c == 3 and 0 <= q - 1 < PAIRS:
                                copy_max(q - 1)
                            if c == 3 and LEAD <= q + 3 < PAIRS:
                                float_copy(q + 3)
                        else:
                            if c == 2 and LEAD <= q + 3 < PAIRS:
                                second_part(q + 3)
                        if c == 3 and 0 <= 2 * (q - WEIGHTS_AT) + i < 4:
                            copy_weights(2 * (q - WEIGHTS_AT) + i)
                        at = (q - PAIRS, i, c)
                        if at == (0, 0, 3):
                            normalise(0)
                        if at == (0, 1, 2):
                            copy_xT(0)
                        if at == (1, 0, 0):
                            gate_exp(0)
                        if at == (1, 0, 1):
                            normalise(1)
                        if at == (1, 1, 1):
                            copy_xT(1)
                        if at == (1, 1, 2):
                            x_high(0)
                        if at == (2, 0, 1):
                            normalise(2)

            copy_uT(0)
            gate_exp(1)
            for g in range(GROUPS):
                relu(g, 0)
                if g + 2 < GROUPS:
                    copy_xT(g + 2)
                relu(g, 1)
                if g + 1 < GROUPS:
                    x_high(g + 1)
                relu(g, 2)
                relu(g, 3)
                if g + 3 < GROUPS:
                    normalise(g + 3)
                if g + 1 < GROUPS:
                    copy_uT(g + 1)
                if g + 2 < GROUPS:
                    gate_exp(g + 2)

        @block.tensor
        def _(pe):
            pe.wait_ge(s_pool_const, 6)

            def transpose_weights(k):
                if k == 0:
                    pe.wait_ge(s_w, 16 * 11)
                    pe.wait_ge(s_full, PAIRS - LEAD)
                else:
                    pe.wait_ge(s_wTc, (2, 3, 5, 6)[k - 1])
                if k == 3:
                    pe.transpose(qk_t[:, 0:128], a_in[:, :], ident[:, :])
                    mm = pe.transpose(qk_t[:, 128:UW], gw_in[:, :], ident[0:E, 0:E])
                elif k == 4:
                    pe.wait_ge(s_shift, 2)
                    for c in range(FC):
                        mm = pe.matmul(qk_t[:, 0:D], bi_wide[:, c, :], woT[:, c, :], start=(c == 0), stop=(c == FC - 1))
                else:
                    for c in range(FC):
                        src = (wi_in[:, c, :], wo_in[:, c * 128:(c + 1) * 128],
                               b_in[:, c, :, :].rearrange("p e r -> p (e r)"))[k]
                        mm = pe.transpose(qk_t[:, c * 128:(c + 1) * 128], src, ident[:, :])
                mm.then_inc(s_wT, 1)

            def transpose_k(p):
                pe.wait_ge(s_kperm, p + 1)
                if p > LEAD:
                    pe.wait_ge(s_full, p - LEAD)
                elif p >= 1:
                    pe.wait_ge(s_rest, p)
                for i in range(2):
                    pe.transpose(qk_t[:, 256 + i * 128:256 + (i + 1) * 128], kperm[:, p % 2, i, :], ident[:, :])

            def transpose_q(p):
                pe.wait_ge(s_xhat, 2 * (p + 1))
                for i in range(2):
                    mm = pe.transpose(qk_t[:, i * 128:(i + 1) * 128], xhat[:, p % 2, i, :], ident[:, :])
                mm.then_inc(s_qkT, 1)

            def pass1(n, c):
                i, Q, s = CH * n + c, n // 4, (n // 4) % SLOTS
                if c == 0 and n % 4 == 0:
                    pe.wait_ge(s_stack[s], 16 * STACK_DMAS * (Q // SLOTS + 1))
                    if Q < SLOTS:
                        pe.wait_ge(s_fixed[s], 32)
                if i >= 2:
                    pe.wait_ge(s_max, i - 1)
                q0 = (n % 4) * 128
                for j in range(G):
                    h = c * G + j
                    mm = pe.matmul(sc1[i % 2][:, j * 128:(j + 1) * 128], stack[0:MAX_ROW, s, h, q0:q0 + 128],
                                   stack[0:MAX_ROW, s, h, 512 + q0:640 + q0], start=True, stop=True)
                mm.then_inc(s_sc1, 1)

            def transpose_max(p):
                pe.wait_ge(s_msplit, NMS * (p + 1))
                if p >= 1:
                    pe.wait_ge(s_mTc, p)
                for i in range(2):
                    mm = pe.transpose(bank_max[0:PARTS * H, i * 128:(i + 1) * 128],
                                      max_part[:, p % 2, i, :, :].rearrange("p t h -> p (t h)"), identb[:, :])
                mm.then_inc(s_mT, 1)

            def pass2(n, c):
                i, p, s = CH * n + c, n // 2, (n // 4) % SLOTS
                if c == 0 and n % 2 == 0:
                    pe.wait_ge(s_maxrow[p % 4], 16 * (p // 4 + 1))
                if i >= 2:
                    pe.wait_ge(s_exp, i - 1)
                q0 = (n % 4) * 128
                for j in range(G):
                    h = c * G + j
                    mm = pe.matmul(sc2[i % 2][:, j * 128:(j + 1) * 128], stack[:, s, h, 512 + q0:640 + q0],
                                   stack[:, s, h, q0:q0 + 128], start=True, stop=True)
                mm.then_inc(s_sc2, 1)

            def weigh_v(n, c):
                i = CH * n + c
                if c == 0:
                    pe.wait_ge(s_vpad, 2 * CH + 2 * (n + 1))
                    if n >= 1:
                        pe.wait_ge(s_oc, n)
                pe.wait_ge(s_exp, i + 1)
                c0 = 128 if c == CH - 1 else 0
                for j in range(G):
                    mm = pe.matmul(o_acc[32 * j:32 * j + 32, c0:c0 + 128], v_window(n, c, j),
                                   probs[:, i % 4, j * 128:(j + 1) * 128], start=(c in (0, CH - 1)),
                                   stop=(c >= CH - 2))
                mm.then_inc(s_pv, 1)

            def transpose_o(n):
                pe.wait_ge(s_oc, n + 1)
                if n >= 1:
                    pe.wait_ge(s_norm, NNORM * (n - 1) + 4)
                for i in range(2):
                    mm = pe.transpose(o_t[:, i * 128:(i + 1) * 128], o_rows[:, n % 2, i * 128:(i + 1) * 128], ident[:, :])
                mm.then_inc(s_oT, 1)

            def transpose_x(g):
                pe.wait_ge(s_xh2, GT * (g + 1))
                if g == 0:
                    pe.wait_ge(s_shift, 3)
                elif g == 1:
                    pe.wait_ge(s_xTc, 1)
                elif g >= 2:
                    pe.wait_ge(s_u_lo, 2 * g - 3)
                for t in range(GT):
                    mm = pe.transpose(qk_t[:, t * 128:(t + 1) * 128], xhat2[:, t, :], ident[:, :])
                mm.then_inc(s_xT, 1)

            def lora_and_gates(g):
                pe.wait_ge(s_xTc, g + 1)
                if g >= 1:
                    pe.wait_ge(s_u, 4 * g)
                else:
                    pe.wait_ge(s_max, CH * B)
                for t in range(GT):
                    c0 = (t % 2) * UW
                    mm = pe.matmul(ug_bank(t)[:, c0:c0 + UW], xT[:, g % 2, t * 128:(t + 1) * 128], agT[:, :],
                                   start=True, stop=True)
                mm.then_inc(s_ug, 1)

            def transpose_u(g):
                for i, dst in enumerate((qk_t, o_t)):
                    pe.wait_ge(s_u, 4 * g + 2 * (i + 1))
                    if i == 0:
                        pe.wait_ge(s_xTc, min(g + 2, GROUPS))
                    elif g >= 1:
                        pe.wait_ge(s_u_lo, 2 * g)
                    else:
                        pe.wait_ge(s_norm, NNORM * B)
                    for t in range(GT):
                        mm = pe.transpose(dst[:, t * 128:(t + 1) * 128],
                                          u[:, i, t, :, :].rearrange("p e r -> p (e r)"), ident[:, :])
                    mm.then_inc(s_uT, 1)

            def three(dst, w, v, start, stop, closed=False):
                for k, (a, b) in enumerate(((0, 0), (0, 1), (1, 0))):
                    mm = pe.matmul(dst, w[a], v[b], start=(start and k == 0), stop=(closed or (stop and k == 2)),
                                   skip_group_check=closed)
                return mm

            def first_expert(g, c):
                i = FC * g + c
                if c == 0:
                    pe.wait_ge(s_x_lo, g + 1)
                if i >= 3:
                    pe.wait_ge(s_hs, i - 2)
                three(chunk_bank(i)[:, :], [wi_part[:, k, c, :] for k in range(2)],
                      [x_part[:, g % 2, k, :] for k in range(2)], True, False)
                if c == 0:
                    pe.wait_ge(s_u_lo, 2 * g + 1)
                three(chunk_bank(i)[:, :], [b_part[:, k, c, :] for k in range(2)],
                      [u_part[:, 0, k, :] for k in range(2)], False, True).then_inc(s_a, 1)

            def second_expert(g, c):
                i = FC * g + c
                if c == 0:
                    pe.wait_ge(s_u_lo, 2 * g + 2)
                pe.wait_ge(s_h1, i + 1)
                three(chunk_bank(i)[:, :], [b_part[:, k, c, :] for k in range(2)],
                      [u_part[:, 1, k, :] for k in range(2)], False, True, closed=True).then_inc(s_d, 1)

            def out_weights(g):
                pe.wait_ge(s_hs, FC * (g + 1))
                if g >= 1:
                    pe.wait_ge(s_fin, NFIN * g)
                for t in range(GT):
                    for c in range(FC):
                        mm = pe.matmul(bank_out[:, t * 128:(t + 1) * 128], hsum[:, c, t * 128:(t + 1) * 128], woT[:, c, :],
                                       start=(c == 0), stop=(c == FC - 1))
                mm.then_inc(s_o, 1)

            def behind(j):
                if 0 <= j < CH * B:
                    weigh_v(j // CH, j % CH)

            for p in range(LEAD):
                transpose_k(p)
                transpose_q(p)

            for q in range(PAIRS + 3):
                for i in range(2):
                    m, n = 2 * q + i, 2 * (q - 2) + i
                    for c in range(CH):
                        if 0 <= m < B:
                            pass1(m, c)
                        if c == 3:
                            behind(CH * n)
                        if 0 <= n < B:
                            pass2(n, c)
                        if i == 0:
                            if c == 0 and LEAD <= q + 3 < PAIRS:
                                transpose_k(q + 3)
                            if c == 2 and LEAD <= q + 3 < PAIRS:
                                transpose_q(q + 3)
                        if c == 3 and 0 <= n - 1 < B:
                            transpose_o(n - 1)
                        if c != 2:
                            behind(CH * n + c - 2)
                        if i == 0 and c == 1 and 0 <= q - 1 < PAIRS:
                            transpose_max(q - 1)
                        if c == 2 and 0 <= 2 * (q - WEIGHTS_AT) + i < 5:
                            transpose_weights(2 * (q - WEIGHTS_AT) + i)
                        at = (q - PAIRS, i, c)
                        if at == (0, 1, 1):
                            transpose_x(0)
                        if at == (0, 1, 3):
                            lora_and_gates(0)
                        if at == (1, 1, 0):
                            transpose_x(1)

            transpose_u(0)
            lora_and_gates(1)
            pe.wait_ge(s_w_lo, 2)
            for g in range(GROUPS):
                first_expert(g, 0)
                if g + 2 < GROUPS:
                    transpose_x(g + 2)
                first_expert(g, 1)
                second_expert(g, 0)
                first_expert(g, 2)
                second_expert(g, 1)
                first_expert(g, 3)
                second_expert(g, 2)
                if g + 1 < GROUPS:
                    transpose_u(g + 1)
                second_expert(g, 3)
                if g + 2 < GROUPS:
                    lora_and_gates(g + 2)
                out_weights(g)

        @block.vector
        def _(dve):
            def zero(s, quarter):
                dve.memset(words[:, s, H // 4 * quarter:H // 4 * (quarter + 1), :], 0.0).then_inc(s_zero[s], 1)

            def stats1(Q):
                dve.wait_ge(s_x[Q], 16)
                for n in range(4 * Q, 4 * Q + 4):
                    dve.bn_stats(stats[:, n, :], X[:, n, :]).then_inc(s_stat, 1)
                for k in range(4):
                    dve.wait_ge(s_stat, 8 * Q + k + 1)
                    dve.bn_aggr(mv[:, 4 * Q + k, :], stats[:, 4 * Q + k, :]).then_inc(s_stat, 1)

            def stats_of(n):
                if n % 4 == 0:
                    dve.wait_ge(s_x[n // 4], 16)
                dve.bn_stats(stats[:, n, :], X[:, n, :]).then_inc(s_stat, 1)
                dve.wait_ge(s_stat, 2 * n + 1)
                dve.bn_aggr(mv[:, n, :], stats[:, n, :]).then_inc(s_stat, 1)

            def variances1(k):
                lo, hi = BATCHES[k]
                dve.wait_ge(s_stat, 2 * hi)
                dve.tensor_scalar(veps[:, lo:hi], mv[:, lo:hi, 1], EPS, None, ALU.add).then_inc(s_var, 1)

            def scales1(k):
                lo, hi = BATCHES[k]
                dve.wait_ge(s_pow, k + 1)
                dve.wait_ge(s_dve_const, 1)
                dve.tensor_tensor(qmul[:, lo:hi], rstd[:, lo:hi], qscale[:, lo:hi], ALU.mult).then_inc(s_scale, 1)
                dve.wait_ge(s_scale, 2 * k + 1)
                dve.scalar_tensor_tensor(out=qadd[:, lo:hi], in0=mv[:, lo:hi, 0], scalar=-1.0, in1=qmul[:, lo:hi],
                                         op0=ALU.mult, op1=ALU.mult).then_inc(s_scale, 1)

            def first_rest(p):
                dve.wait_ge(s_t1, p + 1)
                if p >= 1:
                    dve.wait_ge(s_t2, p)
                    dve.wait_ge(s_t3, p)
                dve.tensor_tensor(halves(rest), halves(qk_t), pair_cols(part[0], p), ALU.subtract).then_inc(s_rest, 1)

            def third_part(p):
                dve.wait_ge(s_t2, p + 1)
                dve.tensor_tensor(pair_cols(part[2], p), halves(rest), pair_cols(part[1], p),
                                  ALU.subtract).then_inc(s_t3, 1)

            zero(0, 0)
            zero(0, 1)
            stats1(0)
            variances1(0)
            dve.wait_ge(s_seq, 32)
            dve.tensor_scalar(qscale[:, :], seq_row[:, :], 0.0, float(DH) ** -0.5, ALU.is_gt,
                              ALU.mult).then_inc(s_dve_const, 1)
            stats1(1)
            scales1(0)
            variances1(1)
            dve.wait_ge(s_b, 16)
            dve.tensor_copy(seq_colf[:, :], seq_col[:, :]).then_inc(s_bias, 1)
            dve.wait_ge(s_pool_const, 8)
            dve.wait_ge(s_bias, 1)
            dve.tensor_scalar(mask_rows[:, :], key_id[:, :], seq_colf[:, 0:1], MASK, ALU.is_ge,
                              ALU.mult).then_inc(s_bias, 1)
            dve.wait_ge(s_bias, 2)
            dve.tensor_tensor(bias_rows[:, :], mask_rows[:, :], b_rows[:, :], ALU.add).then_inc(s_bias, 1)
            dve.wait_ge(s_bias, 3)
            dve.tensor_copy(bias_part[:, 0, :], bias_rows[:, :]).then_inc(s_bias, 1)
            dve.wait_ge(s_bias, 4)
            dve.tensor_tensor(bias_rest[:, :], bias_rows[:, :], bias_part[:, 0, :], ALU.subtract).then_inc(s_bias, 1)
            dve.wait_ge(s_bias, 5)
            dve.tensor_copy(bias_part[:, 1, :], bias_rest[:, :]).then_inc(s_dve_const, 1)
            dve.wait_ge(s_dve_const, 2)
            dve.tensor_tensor(bias_part[:, 2, :], bias_rest[:, :], bias_part[:, 1, :], ALU.subtract).then_inc(s_bias, 1)

            scales1(1)
            for p in range(LEAD):
                first_rest(p)
                if p < 2:
                    stats1(2 + p)
                third_part(p)
                if p == 1:
                    variances1(2)
            scales1(2)

            def row_max(n, c):
                i, p = CH * n + c, n // 2
                dve.wait_ge(s_sc1, i + 1)
                dve.tensor_reduce(negmax[:, p % 2, n % 2, c * G:(c + 1) * G], bank_cols(sc1[i % 2]), AX.X, ALU.max,
                                  negate=True).then_inc(s_max, 1)

            def split_max(p, step):
                o = NMS * p
                src = negmax[:, p % 2, :, :]
                dst = max_part[:, p % 2, :, :, :]
                if step == 0:
                    dve.wait_ge(s_max, 2 * CH * (p + 1))
                    if p >= 2:
                        dve.wait_ge(s_mT, p - 1)
                    dve.tensor_copy(dst[:, :, 0, :], src).then_inc(s_msplit, 1)
                elif step == 1:
                    dve.wait_ge(s_msplit, o + 1)
                    dve.tensor_tensor(max_rest[:, :, :], src, dst[:, :, 0, :], ALU.subtract).then_inc(s_msplit, 1)
                elif step == 2:
                    dve.wait_ge(s_msplit, o + 2)
                    dve.tensor_copy(dst[:, :, 1, :], max_rest[:, :, :]).then_inc(s_msplit, 1)
                else:
                    dve.wait_ge(s_msplit, o + 3)
                    dve.tensor_tensor(dst[:, :, 2, :], max_rest[:, :, :], dst[:, :, 1, :],
                                      ALU.subtract).then_inc(s_msplit, 1)

            def add_attention(n, step):
                o = NNORM * n
                C3 = CH - 1
                a = o_t[:, 0:128].rearrange("p (g w) -> p g w", g=G)
                z = o_t[:, 128:256].rearrange("p (g w) -> p g w", g=G)
                sums = a[:, :, 0:9 * C3].rearrange("p g (c w) -> p c g w", c=C3)
                rs = rsum[:, n % 2, :, :]
                on = o_norm[:, n % 2, :, :, :]
                if step == 0:
                    dve.wait_ge(s_oT, n + 1)
                    dve.reciprocal(rs[:, 0:C3, :], sums[:, :, :, DH]).then_inc(s_norm, 1)
                elif step == 1:
                    dve.reciprocal(rs[:, C3, :], z[:, :, DH]).then_inc(s_norm, 1)
                elif step == 2:
                    dve.wait_ge(s_norm, o + 2)
                    dve.tensor_tensor(on[:, 0:C3, :, :], sums[:, :, :, 0:DH],
                                      rs[:, 0:C3, :, None].to_broadcast([128, C3, G, DH]), ALU.mult).then_inc(s_norm, 1)
                    dve.tensor_tensor(on[:, C3, :, :], z[:, :, 0:DH],
                                      rs[:, C3, :, None].to_broadcast([128, G, DH]), ALU.mult).then_inc(s_norm, 1)
                else:
                    if n == 0:
                        dve.wait_ge(s_tanh, 1)
                    dve.wait_ge(s_norm, o + 4)
                    dve.scalar_tensor_tensor(out=X[:, n, :], in0=on.rearrange("p c g d -> p (c g d)"),
                                             scalar=tanh_g[:, 0:1], in1=X[:, n, :], op0=ALU.mult,
                                             op1=ALU.add).then_inc(s_norm, 1)

            def stats2_of(g):
                o = NST2 * g
                if g >= 1:
                    dve.wait_ge(s_xh2, GT * g)
                for t in range(GT):
                    dve.bn_stats(stats2[:, t, :], X[:, GT * g + t, :]).then_inc(s_stat2, 1)
                for t in range(GT):
                    dve.wait_ge(s_stat2, o + t + 1)
                    dve.bn_aggr(mv2[:, t, :], stats2[:, t, :]).then_inc(s_stat2, 1)
                dve.wait_ge(s_stat2, o + 8)
                dve.tensor_scalar(veps2[:, :], mv2[:, :, 1], EPS, None, ALU.add).then_inc(s_stat2, 1)

            def shifts2(g):
                dve.wait_ge(s_pow2, g + 1)
                dve.scalar_tensor_tensor(out=nmean2[:, :], in0=mv2[:, :, 0], scalar=-1.0, in1=rstd2[:, :],
                                         op0=ALU.mult, op1=ALU.mult).then_inc(s_stat2, 1)

            def wide(t):
                return t[:, :, None].to_broadcast([128, GT, E])

            steps = [0]

            def gate_step(ins):
                steps[0] += 1
                ins.then_inc(s_gate, 1)

            def last_step():
                dve.wait_ge(s_gate, steps[0])

            def gates_shift(g):
                dve.wait_ge(s_ug, g + 1)
                if g >= 1:
                    last_step()
                for i in range(2):
                    src = ug_bank(2 * i)[:, 0:2 * UW].rearrange("p (t w) -> p t w", t=2)[:, :, E * R:UW]
                    gate_step(dve.tensor_tensor(lg[:, 2 * i:2 * i + 2, :], src,
                                                gb_rows[:, None, :].to_broadcast([128, 2, E]), ALU.add))
                last_step()
                gate_step(dve.tensor_reduce(lmax[:, :], lg[:, :, :], AX.X, ALU.max))
                last_step()
                if g >= 1:
                    dve.wait_ge(s_gexp, g)
                gate_step(dve.tensor_tensor(lsh[:, :, :], lg[:, :, :], wide(lmax), ALU.subtract))

            def gates_score(g):
                dve.wait_ge(s_gexp, g + 1)
                gate_step(dve.tensor_reduce(lsum[:, :], lexp[:, :, :], AX.X, ALU.add))
                last_step()
                gate_step(dve.reciprocal(lmax[:, :], lsum[:, :]))
                last_step()
                gate_step(dve.tensor_tensor(score[:, :, :], lexp[:, :, :], wide(lmax), ALU.mult))

            def gates_top(i):
                last_step()
                gate_step(dve.tensor_reduce(top[:, i, :], score[:, :, :], AX.X, ALU.max))
                last_step()
                gate_step(dve.tensor_tensor(tie[:, :, :], score[:, :, :], wide(top[:, i, :]), ALU.is_equal))

            def gates_pick(i):
                last_step()
                gate_step(dve.tensor_tensor(lg[:, :, :], tie[:, :, :],
                                            first[:, None, :].to_broadcast([128, GT, E]), ALU.mult))
                last_step()
                gate_step(dve.tensor_reduce(key[:, :], lg[:, :, :], AX.X, ALU.max))
                last_step()
                gate_step(dve.tensor_tensor(hot[:, i, :, :], lg[:, :, :], wide(key), ALU.is_equal))

            def gates_drop():
                last_step()
                gate_step(dve.scalar_tensor_tensor(
                    out=score[:, :, :].rearrange("p t e -> p (t e)"),
                    in0=hot[:, 0, :, :].rearrange("p t e -> p (t e)"), scalar=-2.0,
                    in1=score[:, :, :].rearrange("p t e -> p (t e)"), op0=ALU.mult, op1=ALU.add))

            def gates_end(g):
                gate_step(dve.tensor_tensor(lsum[:, :], top[:, 0, :], top[:, 1, :], ALU.add))
                last_step()
                gate_step(dve.tensor_tensor(hot_diff[:, :, :], hot[:, 1, :, :], hot[:, 0, :, :], ALU.subtract))
                if g >= 2:
                    dve.wait_ge(s_base, g - 1)
                gate_step(dve.tensor_scalar(gate[:, g % 2, :], lsum[:, :], tanh_g[:, 1:2], None, ALU.mult))

            def mask_u(g):
                last_step()
                if g >= 1:
                    dve.wait_ge(s_uT, 2 * g)
                for k, m in enumerate((hot[:, 0, :, :], hot_diff[:, :, :])):
                    for i in range(2):
                        for_tiles = ug_bank(2 * i)[:, 0:2 * UW].rearrange("p (t w) -> p t w", t=2)[:, :, 0:E * R]
                        dve.tensor_tensor(u[:, k, 2 * i:2 * i + 2, :, :],
                                          for_tiles.rearrange("p t (e r) -> p t e r", e=E),
                                          m[:, 2 * i:2 * i + 2, :, None].to_broadcast([128, 2, E, R]),
                                          ALU.mult).then_inc(s_u, 1)

            def sum_experts(g, c):
                i = FC * g + c
                dve.wait_ge(s_d, i + 1)
                dve.scalar_tensor_tensor(out=hsum[:, c, :], in0=chunk_bank(i)[:, :], scalar=nbi_col[:, c:c + 1],
                                         in1=h1[:, c, :], op0=ALU.max, op1=ALU.add).then_inc(s_hs, 1)

            def u_low(g):
                for k, src in enumerate((qk_t, o_t)):
                    dve.wait_ge(s_uTc, 2 * g + k + 1)
                    dve.tensor_tensor(u_part[:, k, 1, :], src[:, :], u_part[:, k, 0, :],
                                      ALU.subtract).then_inc(s_u_lo, 1)

            def finish(g):
                dve.wait_ge(s_base, g + 1)
                if g >= 2:
                    dve.wait_ge(s_out[g % 2], 16 * (g // 2))
                dve.wait_ge(s_o, g + 1)
                for t in range(GT):
                    dve.scalar_tensor_tensor(out=res[:, g % 2, t, :], in0=bank_out[:, t * 128:(t + 1) * 128],
                                             scalar=gate[:, g % 2, t:t + 1], in1=base[:, t, :], op0=ALU.mult,
                                             op1=ALU.add).then_inc(s_fin, 1)

            for q in range(PAIRS + 3):
                for i in range(2):
                    m, n = 2 * q + i, 2 * (q - 2) + i
                    for c in range(CH):
                        if 0 <= m < B:
                            row_max(m, c)
                        o = n - 2
                        if i == 0 and c == 0 and 0 <= q - 1 < PAIRS:
                            split_max(q - 1, 1)
                            if 0 <= o < B:
                                add_attention(o, 0)
                            split_max(q - 1, 2)
                            if 0 <= o < B:
                                add_attention(o, 1)
                            split_max(q - 1, 3)
                        elif c < 3 and 0 <= o < B:
                            if c == 0:
                                add_attention(o, 0)
                                add_attention(o, 1)
                            else:
                                add_attention(o, c + 1)
                        if i == 1 and c == 3 and 0 <= q < PAIRS:
                            split_max(q, 0)
                        if c == 2 and 4 * LEAD + 2 * q + i < B:
                            stats_of(4 * LEAD + 2 * q + i)
                        if i == 0 and c == 2 and q in (4, 8):
                            scales1(2 + q // 4)
                        at = (q - PAIRS, i, c)
                        if at == (0, 0, 0):
                            stats2_of(0)
                        if at == (0, 0, 1):
                            shifts2(0)
                        if at == (0, 1, 0):
                            stats2_of(1)
                        if at == (0, 1, 3):
                            shifts2(1)
                        if at == (1, 0, 0):
                            gates_shift(0)
                        if at == (1, 0, 1):
                            gates_score(0)
                            gates_top(0)
                        if at == (1, 0, 2):
                            gates_pick(0)
                            gates_drop()
                            gates_top(1)
                        if at == (1, 0, 3):
                            gates_pick(1)
                            gates_end(0)
                        if at == (1, 1, 0):
                            mask_u(0)
                        if at == (1, 1, 1):
                            stats2_of(2)
                        if at == (1, 1, 2):
                            shifts2(2)
                        if (q, i, c) == (WEIGHTS_AT, 0, 3):
                            dve.wait_ge(s_w, 16 * 11)
                            dve.tensor_scalar(nbi_col[:, :], bi_col[:, :], -1.0, None, ALU.mult).then_inc(s_shift, 1)
                            dve.tensor_copy(bi_wide[:, :, :],
                                            bi_col[:, :, None].to_broadcast([128, FC, 128])).then_inc(s_shift, 1)
                        if (q, i, c) == (WEIGHTS_AT + 2, 1, 0):
                            dve.wait_ge(s_wT, 5)
                            dve.scalar_tensor_tensor(out=shift[:, :], in0=bo_rows[:, :], scalar=2.0, in1=qk_t[:, 0:D],
                                                     op0=ALU.mult, op1=ALU.add).then_inc(s_shift, 1)
                if q in (3, 7):
                    variances1(3 + q // 4)

            def gates_of(g):
                gates_shift(g)
                gates_score(g)
                gates_top(0)
                gates_pick(0)
                gates_drop()
                gates_top(1)
                gates_pick(1)
                gates_end(g)

            u_low(0)
            gates_of(1)
            for g in range(GROUPS):
                if g + 1 < GROUPS:
                    mask_u(g + 1)
                sum_experts(g, 0)
                if g + 3 < GROUPS:
                    stats2_of(g + 3)
                sum_experts(g, 1)
                if g + 3 < GROUPS:
                    shifts2(g + 3)
                sum_experts(g, 2)
                sum_experts(g, 3)
                if g + 1 < GROUPS:
                    u_low(g + 1)
                if g + 2 < GROUPS:
                    gates_shift(g + 2)
                    gates_score(g + 2)
                    gates_top(0)
                    gates_pick(0)
                finish(g)
                if g + 2 < GROUPS:
                    gates_drop()
                    gates_top(1)
                    gates_pick(1)
                    gates_end(g + 2)


_INS = ["x", "ctx_2048", "itok_Bx1_68_817", "g_xattn", "g_ffn", "L0_xattn_b", "L0_ffn_wi", "L0_ffn_bi", "L0_ffn_wo",
        "L0_ffn_bo", "L0_ffn_lora_A", "L0_ffn_lora_B", "L0_ffn_gate_w", "L0_ffn_gate_b"]


def kernel(**inputs):
    import numpy as _np
    import concourse.bacc as _bacc
    from concourse import mybir as _mybir
    from concourse.bass_utils import run_bass_kernel_spmd as _run

    nc = _bacc.Bacc("TRN2", target_bir_lowering=False, num_devices=1)
    arrays, args = {}, []
    for name in _INS:
        a = _np.ascontiguousarray(inputs[name])
        arrays[f"in_{name}_dram"] = a
        args.append(nc.dram_tensor(f"in_{name}_dram", a.shape, _mybir.dt.from_np(a.dtype), kind="ExternalInput").ap())
    shape = inputs["x"].shape
    args.append(nc.dram_tensor("out_0_dram", shape, _mybir.dt.float32, kind="ExternalOutput").ap())
    flamingo(nc, *args)
    r = _run(nc, [arrays], core_ids=[0])
    return r.results[0]["out_0_dram"]
```
